# Optimizing a Trainium2 kernel written in Bass

```python
import numpy as np
import jax
import jax.numpy as jnp

def _softmax(x, axis=-1):
    return jax.nn.softmax(x, axis=axis)

def _gelu(x):
    return jax.nn.gelu(x, approximate=True)

def _silu(x):
    return jax.nn.silu(x)

def _sigmoid(x):
    return jax.nn.sigmoid(x)

def _layernorm(x, axis=-1, eps=1e-05):
    m = jnp.mean(x, axis=axis, keepdims=True)
    v = jnp.var(x, axis=axis, keepdims=True)
    return (x - m) / jnp.sqrt(v + eps)

def _scatter_add(tgt, idx, src, axis=0):
    return tgt.at[idx].add(src)

def _segment_sum(src, seg, n):
    return jax.ops.segment_sum(src, seg, n)
kernel_name = 'mk_seq_preln_d1_jaxref_r4_359a02'

def setup_inputs(seed: int=0):
    np.random.seed(seed)
    _w = jnp.asarray

    def _L0_attn_setup():
        import jax, jax.numpy as jnp
        import numpy as np
        D_MODEL = 512
        N_HEADS = 16
        HEAD_DIM = D_MODEL // N_HEADS
        NEG_BIG = -1e+30
        key = jax.random.key(seed)
        ks = jax.random.split(key, 9)
        B, T = (2, 512)
        s_in = 1.0 / np.sqrt(D_MODEL)
        s_hd = 1.0 / np.sqrt(D_MODEL)
        return {'q_input': jax.random.normal(ks[0], (B, T, D_MODEL), dtype=jnp.float32), 'Wq': jax.random.normal(ks[1], (D_MODEL, D_MODEL), dtype=jnp.float32) * s_in, 'bq': jnp.zeros((D_MODEL,), dtype=jnp.float32), 'Wk': jax.random.normal(ks[2], (HEAD_DIM, D_MODEL), dtype=jnp.float32) * s_in, 'bk': jnp.zeros((HEAD_DIM,), dtype=jnp.float32), 'Wv': jax.random.normal(ks[3], (HEAD_DIM, D_MODEL), dtype=jnp.float32) * s_in, 'bv': jnp.zeros((HEAD_DIM,), dtype=jnp.float32), 'Wo': jax.random.normal(ks[4], (D_MODEL, D_MODEL), dtype=jnp.float32) * s_hd, 'bo': jnp.zeros((D_MODEL,), dtype=jnp.float32)}
    _L0_attn_in = _L0_attn_setup()

    def _L0_ffn_setup():
        import jax, jax.numpy as jnp
        import numpy as np
        B, S, D, H = (8, 1024, 512, 1280)

        def ternarize_weight(w):
            abs_mean = jnp.maximum(jnp.mean(jnp.abs(w)), 1e-05)
            thr = 0.7 * abs_mean
            one = jnp.ones((), dtype=w.dtype)
            q = jnp.where(w > thr, one, jnp.where(w < -thr, -one, jnp.zeros((), dtype=w.dtype)))
            return w + jax.lax.stop_gradient(q * abs_mean - w)
        key = jax.random.key(seed)
        k1, k2, k3 = jax.random.split(key, 3)
        x = jax.random.normal(k1, (B, S, D), dtype=jnp.float32)
        w_fc = jax.random.normal(k2, (H, D), dtype=jnp.float32) / np.sqrt(D).astype(np.float32)
        w_proj = jax.random.normal(k3, (D, H), dtype=jnp.float32) / np.sqrt(H).astype(np.float32)
        return {'x': x, 'w_fc': w_fc, 'w_proj': w_proj}
    _L0_ffn_in = _L0_ffn_setup()
    _d = {'L0_attn_q_input': _L0_attn_in['q_input'], 'L0_attn_Wq': _L0_attn_in['Wq'], 'L0_attn_bq': _L0_attn_in['bq'], 'L0_attn_Wk': _L0_attn_in['Wk'], 'L0_attn_bk': _L0_attn_in['bk'], 'L0_attn_Wv': _L0_attn_in['Wv'], 'L0_attn_bv': _L0_attn_in['bv'], 'L0_attn_Wo': _L0_attn_in['Wo'], 'L0_attn_bo': _L0_attn_in['bo'], 'L0_ffn_w_fc': _L0_ffn_in['w_fc'], 'L0_ffn_w_proj': _L0_ffn_in['w_proj']}
    _x0 = _d['L0_attn_q_input']
    _d['L0_attn_q_input'] = jax.random.normal(jax.random.fold_in(jax.random.key(seed), 1), (2, 1024, 512), dtype=_x0.dtype)
    del _x0
    return _d

def reference(L0_attn_q_input, L0_attn_Wq, L0_attn_bq, L0_attn_Wk, L0_attn_bk, L0_attn_Wv, L0_attn_bv, L0_attn_Wo, L0_attn_bo, L0_ffn_w_fc, L0_ffn_w_proj):

    def _L0_attn_ref(q_input, Wq, bq, Wk, bk, Wv, bv, Wo, bo):
        import jax, jax.numpy as jnp
        import numpy as np
        D_MODEL = 512
        N_HEADS = 16
        HEAD_DIM = D_MODEL // N_HEADS
        NEG_BIG = -1e+30
        B, T, _ = q_input.shape
        scale = 1.0 / np.sqrt(HEAD_DIM)
        q = (q_input @ Wq.T + bq).reshape(B, T, N_HEADS, HEAD_DIM).transpose(0, 2, 1, 3)
        k = q_input @ Wk.T + bk
        v = q_input @ Wv.T + bv
        pos = jnp.arange(T)
        mask = pos[None, :] < pos[:, None]
        scores = jnp.einsum('bhtd,bsd->bhts', q, k) * scale
        scores = jnp.where(mask[None, None, :, :], scores, NEG_BIG)
        attn = jax.nn.softmax(scores, axis=-1)
        row_valid = jnp.any(mask, axis=-1)
        attn = attn * row_valid[None, None, :, None].astype(attn.dtype)
        out = jnp.einsum('bhts,bsd->bhtd', attn, v)
        out = out.transpose(0, 2, 1, 3).reshape(B, T, D_MODEL)
        out = out @ Wo.T + bo
        return out

    def _L0_ffn_ref(x, w_fc, w_proj):
        import jax, jax.numpy as jnp
        import numpy as np
        B, S, D, H = (8, 1024, 512, 1280)

        def ternarize_weight(w):
            abs_mean = jnp.maximum(jnp.mean(jnp.abs(w)), 1e-05)
            thr = 0.7 * abs_mean
            one = jnp.ones((), dtype=w.dtype)
            q = jnp.where(w > thr, one, jnp.where(w < -thr, -one, jnp.zeros((), dtype=w.dtype)))
            return w + jax.lax.stop_gradient(q * abs_mean - w)
        h = jnp.einsum('bsd,hd->bsh', x, ternarize_weight(w_fc))
        h = jnp.square(jax.nn.relu(h))
        return jnp.einsum('bsh,dh->bsd', h, ternarize_weight(w_proj))
    x = L0_attn_q_input
    x = x + _L0_attn_ref(_layernorm(x, axis=-1), L0_attn_Wq, L0_attn_bq, L0_attn_Wk, L0_attn_bk, L0_attn_Wv, L0_attn_bv, L0_attn_Wo, L0_attn_bo)
    x = x + _L0_ffn_ref(_layernorm(x, axis=-1), L0_ffn_w_fc, L0_ffn_w_proj)
    return x

_drawn_inputs = setup_inputs


def setup_inputs(seed=0):
    import zlib

    import numpy as np

    out = dict(_drawn_inputs(seed))
    spreads = {'L0_attn_bq': (0.0, 0.8),
     'L0_attn_bk': (0.0, 0.8),
     'L0_attn_bv': (0.0, 0.1),
     'L0_attn_bo': (0.0, 0.1)}
    factors = {}
    for name, (base, spread) in spreads.items():
        noise = np.random.default_rng([zlib.crc32(name.encode()), seed]).standard_normal(out[name].shape)
        drawn = base * np.exp(spread * noise) if base else spread * noise
        out[name] = jnp.asarray(drawn.astype(out[name].dtype))
    for name, factor in factors.items():
        out[name] = (out[name] * factor).astype(out[name].dtype)
    return out
```

```python
import concourse.bass as bass
from concourse import mybir
from concourse.alu_op_type import AluOpType as ALU
from contextlib import ExitStack




def preln_layer(nc, x, Wq, bq, Wk, bk, Wv, bv, Wo, bo, w_fc, w_proj, out):
    f32, f32r = mybir.dt.float32, mybir.dt.float32r
    f16, bf16 = mybir.dt.float16, mybir.dt.bfloat16
    ACT = mybir.ActivationFunctionType
    AXX = mybir.AxisListType.X

    P = 128
    B, T, D = x.shape
    HD = Wk.shape[0]
    H = D // HD
    F = w_fc.shape[0]
    KD = D // P
    KF = F // P
    HG = P // HD
    G = H // HG
    CW = 512
    NCH = T // CW
    TB = T // P
    CT = CW // P
    NT = B * TB
    EPS = 1e-5
    SCALE = float(HD) ** -0.5
    NEG = -1e30
    NEWTON = 3
    LN = 5 + 3 * NEWTON
    i32 = mybir.dt.int32
    assert B == 2 and NCH == 2 and D == CW and HG == 4

    x_t = x.rearrange("b (c t p) d -> (b c) p t d", p=P, t=CT)
    x_tile = x.rearrange("b (t p) d -> (b t) p d", p=P)
    out_t = out.rearrange("b (c t p) d -> (b c) p t d", p=P, t=CT)

    PEAKS = []
    for i in range(TB):
        for s0 in range(0, P * (i + 1), CW):
            w = min(CW, P * (i + 1) - s0)
            nh = max(1, min(HG, CW // w))
            for h0 in range(0, HG, nh):
                PEAKS.append((h0, nh, i, s0, w, s0 + w == P * (i + 1)))
    NP = len(PEAKS)
    NPS = NP + 2
    STEPS = []
    for c in range(NCH):
        for j in range(CT * (c + 1)):
            t0 = max(c * CW, j * P)
            STEPS.append((c, j, t0, (c + 1) * CW - t0, j * P >= c * CW))
    NS = len(STEPS)
    NH = 2 * NS
    ND = sum(s[4] for s in STEPS)
    NQ = 3 * HG

    def unit_order(with_peaks):
        ev, done, todo = [], 0.0, list(enumerate(PEAKS)) if with_peaks else []
        whole = sum(s[3] for s in STEPS) * 1.0
        peak_whole = sum(p[1] * p[4] + (P if p[5] else 0) * p[1] for p in PEAKS) * 1.0
        sent, closed = 0.0, not with_peaks

        def peaks():
            nonlocal sent, closed
            f = (done / whole - 0.10) / 0.72
            while todo and sent / peak_whole <= f:
                k, p = todo.pop(0)
                ev.append(("peak", k))
                sent += p[1] * p[4] + (P if p[5] else 0) * p[1]
            if not todo and not closed and done / whole > 0.86:
                ev.append(("turn",))
                closed = True

        for n, s in enumerate(STEPS):
            ev.append(("score", n, 0))
            done += 0.2 * s[3]
            peaks()
            ev.append(("score", n, 1))
            done += 0.2 * s[3]
            peaks()
            if n:
                ev.append(("value", n - 1))
                done += 0.6 * STEPS[n - 1][3]
                if STEPS[n - 1][0] != s[0]:
                    ev.append(("norm", STEPS[n - 1][0]))
                peaks()
        ev.append(("value", NS - 1))
        ev.append(("norm", NCH - 1))
        assert not todo and closed
        return ev

    ctx = ExitStack()
    with ctx:
        def sb(name, shape, dt, stack=ctx):
            return stack.enter_context(nc.sbuf_tensor(name, shape, dt))

        def sem(name):
            return ctx.enter_context(nc.semaphore(name))

        q_hi = sb("q_hi", [P, B * G, T], f32r)
        q_lo = sb("q_lo", [P, B * G, T], f32r)
        k_stack = sb("k_stack", [3 * HD + 2, B, T], f32r)
        v_nat = sb("v_nat", [P, B, TB, HD], f32)
        wo_hi = sb("wo_hi", [P, KD, D], f32r)
        wo_lo = sb("wo_lo", [P, KD, D], f32r)
        fc_T = sb("fc_T", [P, KD, F], f16)
        proj_T = sb("proj_T", [P, KF, D], f16)
        bo_all = sb("bo_all", [P, D], f32)
        ident = sb("ident", [P, P], f32)
        ident16 = sb("ident16", [P, P], f16)
        identb = sb("identb", [P, P], bf16)
        mask_first = sb("mask_first", [P, P], bf16)
        mask = sb("mask", [P, P], bf16)
        ones = sb("ones", [P, P], f32)
        bias_q = sb("bias_q", [P, G], f32)
        bias_kv = sb("bias_kv", [2 * HD, 1], f32)
        stats = sb("stats", [P, CT, 6], f32)
        moments = sb("moments", [P, CT, 2], f32)
        rstd = sb("rstd", [P, CT], f32)
        var = sb("var", [P, CT], f32)
        guess = sb("guess", [P, CT], i32)
        newton = sb("newton", [P, CT], f32)
        w_sum = sb("w_sum", [P, 2], f32)
        w_mean = sb("w_mean", [P, 2], f32)
        w_thr = sb("w_thr", [P, 4], f32)
        out_scale = sb("out_scale", [P, 2], f32)

        with ExitStack() as st:
            zT_hi = sb("zT_hi", [P, NCH, KD, CW], f32r, st)
            zT_lo = sb("zT_lo", [P, NCH, KD, CW], f32r, st)
            w_stage = sb("w_stage", [P, F * KD], f32, st)
            wq_hi = sb("wq_hi", [P, KD, D], f32r, st)
            wq_lo = sb("wq_lo", [P, KD, D], f32r, st)
            wkv_hi = sb("wkv_hi", [P, KD, 2 * HD], f32r, st)
            wkv_lo = sb("wkv_lo", [P, KD, 2 * HD], f32r, st)
            x_in = sb("x_in", [P, 1, CT, D], f32, st)
            w_neg = sb("w_neg", [P, 2, 640], f16, st)
            w_q16 = sb("w_q16", [P, 2, 640], f16, st)
            kv_st = sb("kv_st", [2 * HD, 2, CW], f32r, st)
            v_st = sb("v_st", [HD, CW], f32, st)
        with ExitStack() as st:
            x2 = sb("x2", [P, NT, D], f32, st)
            with ExitStack() as st2:
                q_stack = sb("q_stack", [3 * HD + 2, B, HG, T], f32r, st2)
                prob = sb("prob", [P, 3, HG, CW], f32, st2)
                den = sb("den", [P, CW], f32, st2)
                head_out = sb("head_out", [P, CW], f32, st2)
                peak_a = sb("peak_a", [P, HG, TB], f32, st2)
                peak_b = sb("peak_b", [P, HG, TB - CT], f32, st2)
                peak_t = sb("peak_t", [HG * TB, 2, P], f32r, st2)
            with ExitStack() as st2:
                z2 = sb("z2", [P, CT, D], f32, st2)
                z2T_hi = sb("z2T_hi", [P, KD, CW], f16, st2)
                z2T_lo = sb("z2T_lo", [P, KD, CW], f16, st2)
                act_hi = sb("act_hi", [P, KF, CW], f16, st2)
                act_lo = sb("act_lo", [P, KF, CW], f16, st2)
                relu_s = sb("relu_s", [P, 2, CW], f32, st2)
                sq_s = sb("sq_s", [P, 2, CW], f32, st2)
                out_s = sb("out_s", [P, 2, D], f32, st2)
        ps = ctx.enter_context(nc.psum_tensor("ps", [P, 8, CW], f32))

        wq_n = w_stage[:, 0:KD * D].rearrange("p (t d) -> p t d", t=KD)
        wo_n = w_stage[:, KD * D:2 * KD * D].rearrange("p (t d) -> p t d", t=KD)
        wkv_n = w_stage[0:2 * HD, 2 * KD * D:2 * KD * D + D]
        fc_n = w_stage[:, :].rearrange("p (t d) -> p t d", t=KF)
        proj_n = w_stage[:, :].rearrange("p (t f) -> p t f", t=KD)

        w_in = [sem(f"w_in{i}") for i in range(3)]
        bias_in = sem("bias_in")
        x_in_s = sem("x_in_s")
        const_ok = sem("const_ok")
        den_ok = sem("den_ok")
        turned = sem("turned")
        passed = sem("passed")
        ln_seq = sem("ln_seq")
        dve_seq = sem("dve_seq")
        pool_seq = sem("pool_seq")
        wt_ready = sem("wt_ready")
        wt_hi = sem("wt_hi")
        wt_free = sem("wt_free")
        tern_sum = sem("tern_sum")
        tern_tot = sem("tern_tot")
        tern_thr = sem("tern_thr")
        tern_neg = sem("tern_neg")
        tern_q = sem("tern_q")
        tern_t = sem("tern_t")
        tern_done = sem("tern_done")
        z_ready = sem("z_ready")
        xt_ready = sem("xt_ready")
        xt_hi = sem("xt_hi")
        xt_free = sem("xt_free")
        pj_ready = sem("pj_ready")
        pj_hi = sem("pj_hi")
        pj_free = sem("pj_free")
        vt_ready = sem("vt_ready")
        vt_done = sem("vt_done")
        k_in = sem("k_in")
        q_in = sem("q_in")
        peak_ready = sem("peak_ready")
        peak_free = sem("peak_free")
        peaks_all = sem("peaks_all")
        peak_in = sem("peak_in")
        score_ready = sem("score_ready")
        exp_done = sem("exp_done")
        mask_done = sem("mask_done")
        value_done = sem("value_done")
        acc_free = sem("acc_free")
        split_done = sem("split_done")
        wo_ready = sem("wo_ready")
        x2_ready = sem("x2_ready")
        x2_in = [sem(f"x2_in{i}") for i in range(B * NCH)]
        x2_bias = sem("x2_bias")
        z2_ready = sem("z2_ready")
        t2_ready = sem("t2_ready")
        t2_hi = sem("t2_hi")
        t2_free = sem("t2_free")
        fc_ready = sem("fc_ready")
        relu_ok = sem("relu_ok")
        sq_ok = sem("sq_ok")
        act_hi_ok = sem("act_hi_ok")
        act_ok = sem("act_ok")
        pr_ready = sem("pr_ready")
        out_ok = sem("out_ok")
        out_in = [sem("out_in0"), sem("out_in1")]

        TP, PJ, WT, VT = (0, 1), (2, 3), (4, 5), 6
        PK, SC, AC, DN = (0, 1), (2, 4), 6, 7
        CRED = 2
        PCRED = 3

        pieces = [("fc", i) for i in range(KF)] + [("proj", i) for i in range(2 * KD)]
        HF = F // 2

        def piece(n, buf):
            kind, i = pieces[n]
            if kind == "fc":
                return fc_n[:, i, :], buf[:, n % 2, 0:D], KD
            return proj_n[:, i // 2, (i % 2) * HF:(i % 2 + 1) * HF], buf[:, n % 2, 0:HF], KF // 2

        block = ctx.enter_context(nc.Block())

        @block.sync
        def _(sp):
            sp.dma_start(x_in[:, 0, :, :], x_t[0, :, :, :]).then_inc(x_in_s, 16)
            sp.dma_start(wq_n, Wq.rearrange("(t p) d -> p t d", p=P)).then_inc(w_in[0], 16)
            sp.dma_start(wkv_n[0:HD, :], Wv).then_inc(w_in[0], 16)
            sp.dma_start(wkv_n[HD:2 * HD, :], Wk).then_inc(w_in[0], 16)
            sp.dma_start(wo_n, Wo.rearrange("(t p) d -> p t d", p=P)).then_inc(w_in[0], 16)
            sp.dma_start(bias_q[:, :], bq.rearrange("(g p) -> p g", p=P), allow_slow_non_contiguous=True).then_inc(bias_in, 16)
            sp.dma_start(bias_kv[0:HD, :], bv.rearrange("(p o) -> p o", o=1)).then_inc(bias_in, 16)
            sp.dma_start(bias_kv[HD:2 * HD, :], bk.rearrange("(p o) -> p o", o=1)).then_inc(bias_in, 16)
            sp.dma_start(bo_all[:, :], bo.rearrange("(o d) -> o d", o=1).broadcast_to([P, D])).then_inc(bias_in, 16)
            sp.wait_ge(wt_ready, 2 * KD + 1)
            sp.dma_start(fc_n, w_fc.rearrange("(t p) d -> p t d", p=P)).then_inc(w_in[1], 16)

            def chunk(b, c):
                sp.wait_ge(xt_ready, CT * (2 * b + c + 1))
                sp.dma_start(x_in[:, 0, :, :], x_t[2 * b + c + 1, :, :, :]).then_inc(x_in_s, 16)

            def keys(b, c):
                sp.wait_ge(pj_free, CRED + (G + 1) * (2 * b + c + 1))
                for row, part in ((0, 0), (HD, 1), (2 * HD, 0)):
                    sp.dma_start(k_stack[row:row + HD, b, c * CW:(c + 1) * CW].bitcast(f32),
                                 kv_st[HD:2 * HD, part, :].bitcast(f32)).then_inc(k_in, 16)

            with sp.Fori(0, B - 1) as b:
                for c in range(NCH):
                    chunk(b, c)
                    keys(b, c)
            chunk(B - 1, 0)
            keys(B - 1, 0)
            keys(B - 1, 1)
            sp.wait_ge(tern_q, KF)
            sp.dma_start(proj_n, w_proj.rearrange("(t p) f -> p t f", p=P)).then_inc(w_in[2], 16)

            def query_rows(g, b):
                for h in range(HG):
                    for row, part in ((0, q_hi), (HD, q_hi), (2 * HD, q_lo)):
                        sp.dma_start(q_stack[row:row + HD, b, h, :].bitcast(f32),
                                     part[h * HD:(h + 1) * HD, b * G + g, :].bitcast(f32)).then_inc(q_in, 16)

            def peak_rows_in(n, b):
                sp.wait_ge(peak_free, CRED + NPS * (n + 1))
                for part in range(2):
                    row = q_stack[3 * HD + part:3 * HD + part + 1, b, :, :].bitcast(f32)
                    sp.dma_start(row.rearrange("o h (i p) -> o (h i) p", p=P),
                                 peak_t[:, part, :].bitcast(f32)).then_inc(peak_in, 16)

            sp.wait_ge(pj_free, CRED + (G + 1) * 2 * B)
            sp.wait_ge(vt_done, NCH * B)
            sp.wait_ge(tern_done, len(pieces))
            query_rows(0, 0)
            peak_rows_in(0, 0)
            with sp.Fori(0, G - 1) as g:
                for b in range(B):
                    n = 2 * g + b
                    sp.wait_ge(score_ready, NH * n)
                    query_rows(g + b, 1 - b)
                    peak_rows_in(n + 1, 1 - b)
            sp.wait_ge(score_ready, NH * 2 * (G - 1))
            query_rows(G - 1, 1)
            peak_rows_in(2 * G - 1, 1)
            for tl in range(0, NT, CT):
                sp.dma_start(x2[:, tl:tl + CT, :], x_t[tl // CT, :, :, :]).then_inc(x2_in[tl // CT], 16)

            with sp.Fori(0, B * NCH) as ch:
                for t in range(CT):
                    sp.wait_ge(out_ok, CRED + CT * ch + t + 1)
                    sp.dma_start(out_t[ch, :, t, :], out_s[:, t % 2, :]).then_inc(out_in[t % 2], 16)
            sp.wait_ge(out_in[0], 16 * NT // 2)
            sp.wait_ge(out_in[1], 16 * NT // 2)

        @block.gpsimd
        def _(pool):
            n_seq = [0]

            def link(ins):
                n_seq[0] += 1
                ins.then_inc(pool_seq, 1)
                pool.wait_ge(pool_seq, n_seq[0])

            for m in (ident, ident16, identb):
                link(nc.gpsimd.memset(m[:, :], 0.0))
                nc.gpsimd.affine_select(out=m[:, :], in_=m[:, :], compare_op=ALU.not_equal, fill=1.0, base=0,
                                        pattern=[[-1, P]], channel_multiplier=1).then_inc(const_ok, 1)
            nc.gpsimd.memset(ones[:, :], 1.0).then_inc(const_ok, 1)
            for m in (mask, mask_first):
                link(nc.gpsimd.memset(m[:, :], 0.0))
                ins = nc.gpsimd.affine_select(out=m[:, :], in_=m[:, :], compare_op=ALU.is_gt, fill=NEG, base=0,
                                              pattern=[[-1, P]], channel_multiplier=1)
                if m is mask_first:
                    link(ins)
                    ins = nc.gpsimd.memset(m[0:1, 0:1], 0.0)
                ins.then_inc(const_ok, 1)
            nc.gpsimd.memset(k_stack[3 * HD:3 * HD + 2, :, :].bitcast(f32), 1.0).then_inc(const_ok, 1)

            pool.wait_ge(const_ok, 7)
            for n in range(len(pieces)):
                kind, i = pieces[n]
                if i == 0:
                    pool.wait_ge(tern_thr, 1 + (kind == "proj"))
                src, dst, _ = piece(n, w_neg)
                if n >= 2:
                    pool.wait_ge(tern_q, n - 1)
                k = 2 * (kind == "proj")
                nc.gpsimd.tensor_scalar(dst, src, w_thr[:, k + 1:k + 2], None, ALU.is_lt).then_inc(tern_neg, 1)

            def unit(g, b, with_peaks):
                n = 2 * g + b
                diag = 0
                for ev in unit_order(with_peaks):
                    if ev[0] == "score" and ev[2] == 1 and STEPS[ev[1]][4]:
                        pool.wait_ge(exp_done, CRED + NH * n + 2 * ev[1] + 2)
                        pool.sem_inc(passed, 1)
                        part = prob[:, ev[1] % 3, :, 0:P]
                        nc.gpsimd.affine_select(out=part, in_=part, compare_op=ALU.is_gt, fill=0.0, base=0,
                                                pattern=[[0, HG], [1, P]], channel_multiplier=-1).then_inc(mask_done, 1)
                        diag += 1
                    if ev[0] == "norm":
                        c = ev[1]
                        hi = q_hi[:, b * G + g, c * CW:(c + 1) * CW]
                        lo = q_lo[:, b * G + g, c * CW:(c + 1) * CW]
                        pool.wait_ge(acc_free, 2 * n + c + 1)
                        nc.gpsimd.tensor_copy(hi, head_out[:, :]).then_inc(split_done, 1)
                        pool.wait_ge(split_done, 2 * (2 * n + c) + 1)
                        nc.gpsimd.tensor_tensor(lo, head_out[:, :], hi.bitcast(f32), ALU.subtract).then_inc(split_done, 1)

            with pool.Fori(0, G - 1) as g:
                for b in range(B):
                    unit(g, b, True)
            unit(G - 1, 0, True)
            unit(G - 1, 1, False)

            for tl in range(NT):
                pool.wait_ge(x2_in[tl // CT], 16)
                if tl == 0:
                    pool.wait_ge(bias_in, 64)
                nc.gpsimd.tensor_tensor(x2[:, tl, :], x2[:, tl, :], bo_all[:, :], ALU.add).then_inc(x2_bias, 1)

        @block.tensor
        def _(pe):
            pe.sem_inc(value_done, PCRED)
            pe.wait_ge(const_ok, 1)
            pe.wait_ge(w_in[0], 64)
            for n in range(2 * KD + 1):
                if n >= 2:
                    pe.wait_ge(wt_free, n - 1)
                bank = ps[:, WT[n % 2], :]
                if n == KD:
                    for k in range(KD):
                        ins = nc.tensor.transpose(bank[:, k * 2 * HD:(k + 1) * 2 * HD], wkv_n[:, k * P:(k + 1) * P],
                                                  ident[0:2 * HD, 0:2 * HD])
                else:
                    nat, k = (wq_n, n) if n < KD else (wo_n, n - KD - 1)
                    for t in range(KD):
                        ins = nc.tensor.transpose(bank[:, t * P:(t + 1) * P], nat[:, t, k * P:(k + 1) * P], ident[:, :])
                ins.then_inc(wt_ready, 1)

            def token_tiles(b, c):
                s = 2 * b + c
                pe.wait_ge(z_ready, s + 1)
                for t in range(CT):
                    pe.wait_ge(xt_free, CT * s + t + 1)
                    for k in range(KD):
                        ins = nc.tensor.transpose(ps[:, TP[t % 2], k * P:(k + 1) * P], x_in[:, 0, t, k * P:(k + 1) * P],
                                                  ident[:, :])
                    ins.then_inc(xt_ready, 1)

            def project(b, c):
                s = 2 * b + c
                pe.wait_ge(xt_free, CRED + CT * (s + 1))
                for m in range(G + 1):
                    pe.wait_ge(pj_free, (G + 1) * s + m + 1)
                    if m < G:
                        bank, wh, wl, cols = ps[:, PJ[m % 2], :], wq_hi, wq_lo, slice(m * P, (m + 1) * P)
                    else:
                        bank, wh, wl, cols = ps[0:2 * HD, PJ[m % 2], :], wkv_hi, wkv_lo, slice(0, 2 * HD)
                    terms = [(w, z, k) for w, z in ((wh, zT_hi), (wh, zT_lo), (wl, zT_hi)) for k in range(KD)]
                    for i, (w, z, k) in enumerate(terms):
                        ins = nc.tensor.matmul(bank, w[:, k, cols], z[:, c, k, :], start=i == 0, stop=i == len(terms) - 1)
                    ins.then_inc(pj_ready, 1)

            def values(b, c):
                s = 2 * b + c
                pe.wait_ge(pj_hi, (G + 1) * (s + 1))
                pe.wait_ge(vt_done, s)
                pe.sem_inc(passed, 1)
                for t in range(CT):
                    ins = nc.tensor.transpose(ps[:, VT, t * HD:(t + 1) * HD], v_st[:, t * P:(t + 1) * P], ident[0:HD, 0:HD])
                ins.then_inc(vt_ready, 1)

            def ternary(which):
                for n in range(len(pieces)):
                    kind, i = pieces[n]
                    if kind != which:
                        continue
                    if i == 0:
                        pe.wait_ge(const_ok, 4)
                        pe.wait_ge(tern_sum, 1 + (kind == "proj"))
                        k = int(kind == "proj")
                        nc.tensor.matmul(ps[:, 7, k:k + 1], ones[:, :], w_sum[:, k:k + 1], start=True, stop=True).then_inc(tern_tot, 1)
                        pe.wait_ge(wt_free, 2 * KD + 1)
                    pe.wait_ge(tern_q, n + 1)
                    if n >= 2:
                        pe.wait_ge(tern_done, n - 1)
                    _, src, nb = piece(n, w_q16)
                    bank = ps[:, WT[n % 2], :].bitcast(f16)
                    for k in range(nb):
                        ins = nc.tensor.transpose(bank[:, k * P:(k + 1) * P], src[:, k * P:(k + 1) * P], ident16[:, :])
                    ins.then_inc(tern_t, 1)

            pe.wait_ge(wt_free, KD + 1)
            with pe.Fori(0, B) as b:
                for c in range(NCH):
                    token_tiles(b, c)
                    project(b, c)
                    values(b, c)
            ternary("fc")
            ternary("proj")

            def peak(n, g, b, k):
                h0, nh, i, s0, w, diagonal = PEAKS[k]
                if k == 0:
                    pe.wait_ge(q_in, 16 * NQ * (n + 1))
                pe.wait_ge(peak_free, NPS * n + k + 1)
                for h in range(h0, h0 + nh):
                    region = ps[:, PK[k % 2], (h - h0) * w:(h - h0 + 1) * w]
                    ins = nc.tensor.matmul(region, q_stack[0:3 * HD, b, h, i * P:(i + 1) * P],
                                           k_stack[0:3 * HD, b, s0:s0 + w], start=True, stop=not diagonal)
                    if diagonal:
                        ins = nc.tensor.matmul(region[:, w - P:w], identb[:, :], (mask if i else mask_first)[:, :],
                                               start=False, stop=True)
                ins.then_inc(peak_ready, 1)

            def turn(n):
                pe.wait_ge(peaks_all, n + 1)
                pe.wait_ge(peak_free, NPS * n + NP + 1)
                nc.tensor.transpose(ps[0:HG * TB, PK[NP % 2], 0:P], peak_a[:, :, :].rearrange("p h i -> p (h i)"),
                                    ident[:, :]).then_inc(peak_ready, 1)

            def unit(g, b, with_peaks):
                n = 2 * g + b
                diag = 0
                for ev in unit_order(with_peaks):
                    if ev[0] == "score":
                        c, j, t0, w, _ = STEPS[ev[1]]
                        if ev[1:] == (0, 0):
                            pe.wait_ge(peak_in, 32 * (n + 1))
                        hs = 2 * ev[1] + ev[2]
                        pe.wait_ge(exp_done, NH * n + hs + 1)
                        for h in range(2):
                            ins = nc.tensor.matmul(ps[:, SC[hs % 2] + h, 0:w], k_stack[:, b, j * P:(j + 1) * P],
                                                   q_stack[:, b, 2 * ev[2] + h, t0:t0 + w], start=True, stop=True)
                        ins.then_inc(score_ready, 1)
                    elif ev[0] == "peak":
                        peak(n + 1, None, 1 - b, ev[1])
                    elif ev[0] == "turn":
                        turn(n + 1)
                    elif ev[0] == "value":
                        c, j, t0, w, diagonal = STEPS[ev[1]]
                        last = j == CT * (c + 1) - 1
                        if diagonal:
                            diag += 1
                            pe.wait_ge(mask_done, ND * n + diag)
                        else:
                            pe.wait_ge(exp_done, CRED + NH * n + 2 * ev[1] + 2)
                        if j == 0:
                            pe.wait_ge(acc_free, 2 * n + c)
                        cols = slice(t0 - c * CW, t0 - c * CW + w)
                        for h in range(HG):
                            nc.tensor.matmul(ps[h * HD:(h + 1) * HD, AC, cols], v_nat[:, b, j, :],
                                             prob[:, ev[1] % 3, h, 0:w], start=j == 0, stop=last)
                        for h in range(HG):
                            ins = nc.tensor.matmul(ps[h * HD:(h + 1) * HD, DN, cols], ones[:, 0:HD],
                                                   prob[:, ev[1] % 3, h, 0:w], start=j == 0, stop=last)
                        ins.then_inc(value_done, 1)

            pe.wait_ge(const_ok, 7)
            pe.wait_ge(k_in, 48 * NCH * B)
            pe.wait_ge(vt_done, NCH * B)
            pe.wait_ge(tern_done, len(pieces))
            pe.wait_ge(pj_free, CRED + (G + 1) * NCH * B)
            for k in range(NP):
                peak(0, 0, 0, k)
            turn(0)
            with pe.Fori(0, G - 1) as g:
                for b in range(B):
                    unit(g, b, True)
            unit(G - 1, 0, True)
            unit(G - 1, 1, False)

            for tl in range(NT):
                b, i = tl // TB, tl % TB
                if tl == 0:
                    pe.wait_ge(split_done, 2 * 2 * 2 * G)
                    pe.wait_ge(acc_free, 2 * 2 * G)
                if tl >= 2:
                    pe.wait_ge(x2_ready, tl - 1)
                terms = [(o, w, g) for o, w in ((q_hi, wo_hi), (q_hi, wo_lo), (q_lo, wo_hi)) for g in range(G)]
                for n, (o, w, g) in enumerate(terms):
                    ins = nc.tensor.matmul(ps[:, 6 + tl % 2, :], o[:, b * G + g, i * P:(i + 1) * P], w[:, g, :],
                                           start=n == 0, stop=n == len(terms) - 1)
                ins.then_inc(wo_ready, 1)

            def token_tiles2(ch):
                pe.wait_ge(z2_ready, ch + 1)
                for t in range(CT):
                    pe.wait_ge(t2_free, CT * ch + t + 1)
                    for k in range(KD):
                        ins = nc.tensor.transpose(ps[:, TP[t % 2], k * P:(k + 1) * P], z2[:, t, k * P:(k + 1) * P], ident[:, :])
                    ins.then_inc(t2_ready, 1)

            def fc(ch):
                pe.wait_ge(t2_free, CRED + CT * (ch + 1))
                for f in range(KF):
                    pe.wait_ge(sq_ok, KF * ch + f + 1)
                    n = 0
                    for z in (z2T_hi, z2T_lo):
                        for k in range(KD):
                            ins = nc.tensor.matmul(ps[:, 2 + f % 2, :], fc_T[:, k, f * P:(f + 1) * P], z[:, k, :],
                                                   start=n == 0, stop=n == 2 * KD - 1)
                            n += 1
                    ins.then_inc(fc_ready, 1)

            def proj(ch):
                for t in range(CT):
                    pe.wait_ge(out_ok, CT * ch + t + 1)
                    for f in range(KF):
                        if t == 0:
                            pe.wait_ge(act_ok, KF * ch + f + 1)
                        for n, a in enumerate((act_hi, act_lo)):
                            ins = nc.tensor.matmul(ps[:, 6 + t % 2, :], a[:, f, t * P:(t + 1) * P], proj_T[:, f, :],
                                                   start=f == 0 and n == 0, stop=f == KF - 1 and n == 1)
                    ins.then_inc(pr_ready, 1)

            pe.wait_ge(peak_free, CRED + NPS * B * G)
            pe.wait_ge(exp_done, CRED + NH * B * G)
            pe.wait_ge(x2_ready, NT)
            token_tiles2(0)
            with pe.Fori(0, B * NCH - 1) as ch:
                fc(ch)
                token_tiles2(ch + 1)
                proj(ch)
            fc(B * NCH - 1)
            proj(B * NCH - 1)

        @block.scalar
        def _(act):
            act.sem_inc(exp_done, CRED)

            def copy(out_ap, in_ap):
                return nc.scalar.activation(out_ap, in_ap, ACT.Copy)

            for n in range(2 * KD + 1):
                act.wait_ge(wt_ready, n + 1)
                if n == KD:
                    copy(wkv_hi[:, :, :].rearrange("p k m -> p (k m)"), ps[:, WT[n % 2], 0:KD * 2 * HD]).then_inc(wt_hi, 1)
                else:
                    dst = wq_hi[:, n, :] if n < KD else wo_hi[:, n - KD - 1, :]
                    copy(dst, ps[:, WT[n % 2], :]).then_inc(wt_hi, 1)
            act.wait_ge(bias_in, 64)

            def chunk(b, c):
                s = 2 * b + c
                for t in range(CT):
                    act.wait_ge(xt_ready, CT * s + t + 1)
                    copy(zT_hi[:, c, :, t * P:(t + 1) * P],
                         ps[:, TP[t % 2], :].rearrange("p (k t) -> p k t", k=KD)).then_inc(xt_hi, 1)
                for m in range(G):
                    act.wait_ge(pj_ready, (G + 1) * s + m + 1)
                    nc.scalar.activation(q_hi[:, b * G + m, c * CW:(c + 1) * CW], ps[:, PJ[m % 2], :], ACT.Identity,
                                         bias=bias_q[:, m:m + 1]).then_inc(pj_hi, 1)
                act.wait_ge(pj_ready, (G + 1) * (s + 1))
                act.wait_ge(vt_ready, s)
                act.wait_ge(k_in, 48 * s)
                bank = ps[:, PJ[G % 2], :]
                nc.scalar.activation(v_st[:, :], bank[0:HD, :], ACT.Identity, bias=bias_kv[0:HD, 0:1])
                nc.scalar.activation(kv_st[HD:2 * HD, 0, :], bank[HD:2 * HD, :], ACT.Identity,
                                     bias=bias_kv[HD:2 * HD, 0:1]).then_inc(pj_hi, 1)
                act.wait_ge(vt_ready, s + 1)
                copy(v_nat[:, b, CT * c:CT * (c + 1), :],
                     ps[:, VT, 0:CT * HD].rearrange("p (t d) -> p t d", t=CT)).then_inc(vt_done, 1)

            with act.Fori(0, B) as b:
                for c in range(NCH):
                    chunk(b, c)

            for n in range(len(pieces)):
                kind, i = pieces[n]
                act.wait_ge(tern_t, n + 1)
                bank = ps[:, WT[n % 2], :].bitcast(f16)
                if kind == "fc":
                    dst, nb = fc_T[:, :, i * P:(i + 1) * P], KD
                else:
                    nb = KF // 2
                    dst = proj_T[:, nb * (i % 2):nb * (i % 2 + 1), (i // 2) * P:(i // 2 + 1) * P]
                copy(dst, bank[:, 0:nb * P].rearrange("p (k t) -> p k t", k=nb)).then_inc(tern_done, 1)

            def unit(g, b, with_peaks):
                n = 2 * g + b
                for ev in unit_order(with_peaks):
                    if ev[0] == "score":
                        w, hs = STEPS[ev[1]][3], 2 * ev[1] + ev[2]
                        if ev[2] == 0:
                            act.wait_ge(value_done, NS * n + ev[1] + 1)
                        act.wait_ge(score_ready, NH * n + hs + 1)
                        nc.scalar.activation(prob[:, ev[1] % 3, 2 * ev[2]:2 * ev[2] + 2, 0:w],
                                             ps[:, SC[hs % 2]:SC[hs % 2] + 2, 0:w], ACT.Exp, scale=SCALE).then_inc(exp_done, 1)

            with act.Fori(0, G - 1) as g:
                for b in range(B):
                    unit(g, b, True)
            unit(G - 1, 0, True)
            unit(G - 1, 1, False)

            def tokens2(ch):
                for t in range(CT):
                    act.wait_ge(t2_ready, CT * ch + t + 1)
                    copy(z2T_hi[:, :, t * P:(t + 1) * P],
                         ps[:, TP[t % 2], :].rearrange("p (k t) -> p k t", k=KD)).then_inc(t2_hi, 1)

            def fc(ch):
                def hi(f):
                    act.wait_ge(sq_ok, CRED + KF * ch + f + 1)
                    copy(act_hi[:, f, :], sq_s[:, f % 2, :]).then_inc(act_hi_ok, 1)

                for f in range(KF):
                    act.wait_ge(fc_ready, KF * ch + f + 1)
                    act.wait_ge(sq_ok, KF * ch + f + 1)
                    nc.scalar.activation(relu_s[:, f % 2, :], ps[:, 2 + f % 2, :], ACT.Relu, scale=0.25).then_inc(relu_ok, 1)
                    if f:
                        hi(f - 1)
                hi(KF - 1)

            tokens2(0)
            with act.Fori(0, B * NCH - 1) as ch:
                fc(ch)
                tokens2(ch + 1)
            fc(B * NCH - 1)

        @block.vector
        def _(dve):
            for m in (xt_free, pj_free, peak_free, t2_free, sq_ok, out_ok):
                dve.sem_inc(m, CRED)

            def minus(out_ap, in_ap, hi_ap):
                return nc.vector.tensor_tensor(out_ap, in_ap, hi_ap, ALU.subtract)

            def layer_norm(src, dst, base):
                for t in range(CT):
                    ins = nc.vector.bn_stats(stats[:, t, :], src(t))
                ins.then_inc(ln_seq, 1)
                dve.wait_ge(ln_seq, base + 1)
                dve.sem_inc(passed, 1)
                for t in range(CT):
                    ins = nc.vector.bn_aggr(moments[:, t, :], stats[:, t, :])
                ins.then_inc(ln_seq, 1)
                dve.wait_ge(ln_seq, base + 2)
                at = [base + 2]

                def step(ins):
                    at[0] += 1
                    ins.then_inc(ln_seq, 1)
                    dve.wait_ge(ln_seq, at[0])

                step(nc.vector.tensor_scalar(var[:, :], moments[:, :, 1], EPS, None, ALU.add))
                step(nc.vector.tensor_scalar(guess[:, :], var[:, :].bitcast(i32), 1, None, ALU.logical_shift_right))
                step(nc.vector.tensor_scalar(rstd[:, :].bitcast(i32), guess[:, :], -1.0, float(0x5F3759DF),
                                             ALU.mult, ALU.add))
                for _ in range(NEWTON):
                    step(nc.vector.tensor_tensor(newton[:, :], rstd[:, :], rstd[:, :], ALU.mult))
                    step(nc.vector.scalar_tensor_tensor(newton[:, :], newton[:, :], -0.5, var[:, :], ALU.mult, ALU.mult))
                    step(nc.vector.scalar_tensor_tensor(rstd[:, :], newton[:, :], 1.5, rstd[:, :], ALU.add, ALU.mult))
                for t in range(CT):
                    ins = nc.vector.tensor_scalar(dst(t), src(t), moments[:, t, 0:1], rstd[:, t:t + 1],
                                                  ALU.subtract, ALU.mult)
                return ins

            def norm1(s):
                dve.wait_ge(x_in_s, 16 * (s + 1))
                layer_norm(lambda t: x_in[:, 0, t, :], lambda t: x_in[:, 0, t, :], LN * s).then_inc(z_ready, 1)

            for n in range(2 * KD + 1):
                dve.wait_ge(wt_hi, n + 1)
                if n == KD:
                    minus(wkv_lo[:, :, :].rearrange("p k m -> p (k m)"), ps[:, WT[n % 2], 0:KD * 2 * HD],
                          wkv_hi[:, :, :].rearrange("p k m -> p (k m)").bitcast(f32)).then_inc(wt_free, 1)
                else:
                    hi, lo, k = (wq_hi, wq_lo, n) if n < KD else (wo_hi, wo_lo, n - KD - 1)
                    minus(lo[:, k, :], ps[:, WT[n % 2], :], hi[:, k, :].bitcast(f32)).then_inc(wt_free, 1)
            norm1(0)
            dve.wait_ge(bias_in, 64)

            def chunk(b, c, following):
                s = 2 * b + c
                for t in range(CT):
                    dve.wait_ge(xt_hi, CT * s + t + 1)
                    cols = slice(t * P, (t + 1) * P)
                    minus(zT_lo[:, c, :, cols], ps[:, TP[t % 2], :].rearrange("p (k t) -> p k t", k=KD),
                          zT_hi[:, c, :, cols].bitcast(f32)).then_inc(xt_free, 1)
                for m in range(G):
                    cols = slice(c * CW, (c + 1) * CW)
                    dve.wait_ge(pj_hi, (G + 1) * s + m + 1)
                    nc.vector.scalar_tensor_tensor(q_lo[:, b * G + m, cols], ps[:, PJ[m % 2], :], bias_q[:, m:m + 1],
                                                   q_hi[:, b * G + m, cols].bitcast(f32), ALU.add,
                                                   ALU.subtract).then_inc(pj_free, 1)
                    if m == 1 and following:
                        norm1(s + 1)
                dve.wait_ge(pj_hi, (G + 1) * (s + 1))
                dve.wait_ge(k_in, 48 * s)
                nc.vector.scalar_tensor_tensor(kv_st[HD:2 * HD, 1, :], ps[HD:2 * HD, PJ[G % 2], :],
                                               bias_kv[HD:2 * HD, 0:1], kv_st[HD:2 * HD, 0, :].bitcast(f32),
                                               ALU.add, ALU.subtract).then_inc(pj_free, 1)

            with dve.Fori(0, B - 1) as b:
                for c in range(NCH):
                    chunk(b, c, True)
            chunk(B - 1, 0, True)
            chunk(B - 1, 1, False)

            n_seq = [0]

            def link(ins):
                n_seq[0] += 1
                ins.then_inc(dve_seq, 1)
                dve.wait_ge(dve_seq, n_seq[0])

            for n in range(len(pieces)):
                kind, i = pieces[n]
                k = int(kind == "proj")
                if i == 0:
                    dve.wait_ge(w_in[1 + k], 16)
                    nc.vector.tensor_reduce(w_sum[:, k:k + 1], w_stage[:, :], AXX, ALU.add,
                                            apply_absolute_value=True).then_inc(tern_sum, 1)
                    dve.wait_ge(tern_tot, 1 + k)
                    link(nc.vector.tensor_scalar(w_mean[:, k:k + 1], ps[:, 7, k:k + 1], 1.0 / (D * F), 1e-5,
                                                 ALU.mult, ALU.max))
                    nc.vector.tensor_scalar(w_thr[:, 2 * k:2 * k + 1], w_mean[:, k:k + 1], 0.7, None, ALU.mult)
                    nc.vector.tensor_scalar(w_thr[:, 2 * k + 1:2 * k + 2], w_mean[:, k:k + 1], -0.7, None,
                                            ALU.mult).then_inc(tern_thr, 1)
                    dve.wait_ge(tern_thr, 1 + k)
                dve.wait_ge(tern_neg, n + 1)
                if n >= 2:
                    dve.wait_ge(tern_t, n - 1)
                src, neg, _ = piece(n, w_neg)
                _, dst, _ = piece(n, w_q16)
                nc.vector.scalar_tensor_tensor(dst, src, w_thr[:, 2 * k:2 * k + 1], neg, ALU.is_gt,
                                               ALU.subtract).then_inc(tern_q, 1)
            link(nc.vector.tensor_scalar(out_scale[:, 1:2], w_mean[:, 0:1], w_mean[:, 0:1], 16.0, ALU.mult, ALU.mult))
            link(nc.vector.tensor_tensor(out_scale[:, 0:1], out_scale[:, 1:2], w_mean[:, 1:2], ALU.mult))

            def peak(n, k):
                h0, nh, i, s0, w, _ = PEAKS[k]
                dve.wait_ge(peak_ready, (NP + 1) * n + k + 1)
                dst = peak_b[:, h0:h0 + nh, i - CT:i - CT + 1] if s0 else peak_a[:, h0:h0 + nh, i:i + 1]
                src = ps[:, PK[k % 2], 0:nh * w].rearrange("p (h w) -> p h w", h=nh)
                nc.vector.tensor_reduce(dst, src, AXX, ALU.max).then_inc(peak_free, 1)

            def turn(n, b):
                dve.wait_ge(peak_free, CRED + NPS * n + NP)
                nc.vector.tensor_tensor(peak_a[:, :, CT:TB], peak_a[:, :, CT:TB], peak_b[:, :, :],
                                        ALU.max).then_inc(peaks_all, 1)
                dve.wait_ge(peak_ready, (NP + 1) * (n + 1))
                src = ps[0:HG * TB, PK[NP % 2], 0:P]
                nc.vector.tensor_scalar(peak_t[:, 0, :], src, -1.0, None, ALU.mult).then_inc(turned, 1)
                dve.wait_ge(turned, n + 1)
                nc.vector.scalar_tensor_tensor(peak_t[:, 1, :], src, -1.0, peak_t[:, 0, :].bitcast(f32), ALU.mult,
                                               ALU.subtract).then_inc(peak_free, 2)

            def unit(g, b, with_peaks):
                n = 2 * g + b
                for ev in unit_order(with_peaks):
                    if ev[0] == "peak":
                        peak(n + 1, ev[1])
                    elif ev[0] == "turn":
                        dve.wait_ge(peak_in, 32 * (n + 1))
                        turn(n + 1, 1 - b)
                    elif ev[0] == "norm":
                        c = ev[1]
                        u = 2 * n + c
                        dve.wait_ge(value_done, PCRED + NS * n + (CT if c == 0 else NS))
                        nc.vector.tensor_scalar(den[:, :], ps[:, DN, :], 1e-30, None, ALU.max).then_inc(den_ok, 1)
                        dve.wait_ge(den_ok, 2 * u + 1)
                        nc.vector.reciprocal(den[:, :], den[:, :]).then_inc(den_ok, 1)
                        dve.wait_ge(den_ok, 2 * u + 2)
                        dve.wait_ge(split_done, 2 * u)
                        nc.vector.tensor_tensor(head_out[:, :], ps[:, AC, :], den[:, :], ALU.mult).then_inc(acc_free, 1)

            for k in range(NP):
                peak(0, k)
            turn(0, 0)
            with dve.Fori(0, G - 1) as g:
                for b in range(B):
                    unit(g, b, True)
            unit(G - 1, 0, True)
            unit(G - 1, 1, False)

            for tl in range(NT):
                dve.wait_ge(wo_ready, tl + 1)
                dve.wait_ge(x2_bias, tl + 1)
                nc.vector.tensor_tensor(x2[:, tl, :], ps[:, 6 + tl % 2, :], x2[:, tl, :], ALU.add).then_inc(x2_ready, 1)

            def norm2(ch):
                dve.wait_ge(x2_ready, CT * (ch + 1))
                dve.wait_ge(t2_ready, CT * ch)
                layer_norm(lambda t: x2[:, CT * ch + t, :], lambda t: z2[:, t, :],
                           LN * B * NCH + LN * ch).then_inc(z2_ready, 1)

            def tokens2(ch):
                for t in range(CT):
                    dve.wait_ge(t2_hi, CT * ch + t + 1)
                    cols = slice(t * P, (t + 1) * P)
                    minus(z2T_lo[:, :, cols], ps[:, TP[t % 2], :].rearrange("p (k t) -> p k t", k=KD),
                          z2T_hi[:, :, cols]).then_inc(t2_free, 1)

            def fc(ch, following):
                def lo(f):
                    dve.wait_ge(act_hi_ok, KF * ch + f + 1)
                    minus(act_lo[:, f, :], sq_s[:, f % 2, :], act_hi[:, f, :]).then_inc(act_ok, 1)

                for f in range(KF):
                    dve.wait_ge(act_ok, KF * ch + max(f - 1, 0))
                    dve.wait_ge(relu_ok, KF * ch + f + 1)
                    nc.vector.scalar_tensor_tensor(sq_s[:, f % 2, :], ps[:, 2 + f % 2, :], 0.25, relu_s[:, f % 2, :],
                                                   ALU.mult, ALU.mult).then_inc(sq_ok, 1)
                    if f:
                        lo(f - 1)
                    if f == KF // 2 and following:
                        norm2(ch + 1)
                lo(KF - 1)

            def outputs(ch):
                for t in range(CT):
                    dve.wait_ge(pr_ready, CT * ch + t + 1)
                    dve.wait_ge(out_in[t % 2], 16 * ((CT // 2) * ch + t // 2))
                    nc.vector.scalar_tensor_tensor(out_s[:, t % 2, :], ps[:, 6 + t % 2, :], out_scale[:, 0:1],
                                                   x2[:, CT * ch + t, :], ALU.mult, ALU.add).then_inc(out_ok, 1)

            norm2(0)
            tokens2(0)
            with dve.Fori(0, B * NCH - 1) as ch:
                fc(ch, True)
                tokens2(ch + 1)
                outputs(ch)
            fc(B * NCH - 1, False)
            outputs(B * NCH - 1)


_INS = ["L0_attn_q_input", "L0_attn_Wq", "L0_attn_bq", "L0_attn_Wk", "L0_attn_bk", "L0_attn_Wv", "L0_attn_bv",
        "L0_attn_Wo", "L0_attn_bo", "L0_ffn_w_fc", "L0_ffn_w_proj"]


def kernel(**inputs):
    import numpy as _np
    import concourse.bacc as _bacc
    from concourse import mybir as _mybir
    from concourse.bass_utils import run_bass_kernel_spmd as _run

    nc = _bacc.Bacc("TRN2", target_bir_lowering=False, num_devices=1)
    arrays, args = {}, []
    for name in _INS:
        a = _np.ascontiguousarray(inputs[name])
        arrays[name + "_dram"] = a
        args.append(nc.dram_tensor(name + "_dram", a.shape, _mybir.dt.from_np(a.dtype), kind="ExternalInput").ap())
    x = arrays["L0_attn_q_input_dram"]
    args.append(nc.dram_tensor("out_dram", x.shape, _mybir.dt.from_np(x.dtype), kind="ExternalOutput").ap())
    preln_layer(nc, *args)
    r = _run(nc, [arrays], core_ids=[0])
    return r.results[0]["out_dram"]
```

```python
import concourse.bass as bass
from concourse import mybir
from concourse.alu_op_type import AluOpType as ALU
from contextlib import ExitStack




def preln_layer(nc, x, Wq, bq, Wk, bk, Wv, bv, Wo, bo, w_fc, w_proj, out):
    f32, f32r = mybir.dt.float32, mybir.dt.float32r
    f16, bf16 = mybir.dt.float16, mybir.dt.bfloat16
    ACT = mybir.ActivationFunctionType
    AXX = mybir.AxisListType.X

    P = 128
    B, T, D = x.shape
    HD = Wk.shape[0]
    H = D // HD
    F = w_fc.shape[0]
    KD = D // P
    KF = F // P
    HG = P // HD
    G = H // HG
    CW = 512
    NCH = T // CW
    TB = T // P
    CT = CW // P
    NT = B * TB
    EPS = 1e-5
    SCALE = float(HD) ** -0.5
    NEG = -1e30
    AHEAD = 2
    START = 0.05
    PACE = 0.95
    NEWTON = 3
    LN = 5 + 3 * NEWTON
    FB = 4
    i32 = mybir.dt.int32
    assert B == 2 and NCH == 2 and D == CW and HG == 4

    x_t = x.rearrange("b (c t p) d -> (b c) p t d", p=P, t=CT)
    x_tile = x.rearrange("b (t p) d -> (b t) p d", p=P)
    out_t = out.rearrange("b (c t p) d -> (b c) p t d", p=P, t=CT)

    PEAKS = []
    for i in range(TB):
        for s0 in range(0, P * (i + 1), CW):
            w = min(CW, P * (i + 1) - s0)
            nh = max(1, min(HG, CW // w))
            for h0 in range(0, HG, nh):
                PEAKS.append((h0, nh, i, s0, w, s0 + w == P * (i + 1)))
    NPA = sum(p[2] < CT for p in PEAKS)
    TURNS = [("peak", k) for k in range(len(PEAKS))] + [("turn", 1)]
    TURNS.insert(NPA + 2, ("turn", 0))
    NP = len(TURNS)
    PEAK_WORK = [PEAKS[a][1] * PEAKS[a][4] + P if kind == "peak" else P for kind, a in TURNS]
    assert NP % 2 == 0
    STEPS = []
    for c in range(NCH):
        for j in range(CT * (c + 1)):
            t0 = max(c * CW, j * P)
            STEPS.append((c, j, t0, (c + 1) * CW - t0, j * P >= c * CW))
    NS = len(STEPS)
    NH = 2 * NS
    ND = sum(s[4] for s in STEPS)
    NQ = 3 * HG
    NINV, NOUT = 4, 3
    OUTPUT_STEPS = [("invert", i) for i in range(NINV)] + [("output", i) for i in range(NOUT)]

    def unit_order(with_peaks, follows=True):
        order, todo = [], list(range(NP)) if with_peaks else []
        whole, done, sent = float(sum(s[3] for s in STEPS)), 0.0, 0.0
        finish = [(kind, part, NCH - 1, 1) for kind, part in OUTPUT_STEPS] if follows else []

        def peaks():
            nonlocal sent
            while todo and (len(todo) > 1 or done / whole > 0.97):
                if len(todo) > 1 and sent / sum(PEAK_WORK) > START + done / whole / PACE:
                    break
                m = todo.pop(0)
                order.append((*TURNS[m], m))
                sent += PEAK_WORK[m]

        def value(n):
            nonlocal done
            order.append(("value", n))
            done += 0.4 * STEPS[n][3]
            if n == NS - 1 or STEPS[n + 1][0] != STEPS[n][0]:
                c = STEPS[n][0]
                order.append(("sums", c))
                if c < NCH - 1:
                    finish.extend((kind, part, c, 0) for kind, part in OUTPUT_STEPS)

        for n, s in enumerate(STEPS):
            for half in range(2):
                order.append(("score", n, half))
                done += 0.3 * s[3]
                if finish and (finish[0][0] == "invert" or half):
                    order.append(finish.pop(0))
                peaks()
            if n >= AHEAD:
                value(n - AHEAD)
                peaks()
        for n in range(NS - AHEAD, NS):
            value(n)
            peaks()
        assert not todo and not finish
        return order

    ctx = ExitStack()
    with ctx:
        def sb(name, shape, dt, stack=ctx):
            return stack.enter_context(nc.sbuf_tensor(name, shape, dt))

        def sem(name):
            return ctx.enter_context(nc.semaphore(name))

        k_stack = sb("k_stack", [3 * HD + 2, B, T], f32r)
        v_nat = sb("v_nat", [P, B, TB, HD], f32)
        wo_hi = sb("wo_hi", [P, KD, D], f32r)
        wo_lo = sb("wo_lo", [P, KD, D], f32r)
        w_T = sb("w_T", [P, 2, KF, D], f16)
        bo_all = sb("bo_all", [P, D], f32)
        ident = sb("ident", [P, P], f32)
        ident16 = sb("ident16", [P, P], f16)
        identb = sb("identb", [P, P], bf16)
        mask_first = sb("mask_first", [P, P], bf16)
        mask = sb("mask", [P, P], bf16)
        ones = sb("ones", [P, P], f32)
        bias_q = sb("bias_q", [P, G], f32)
        bias_kv = sb("bias_kv", [2 * HD, 1], f32)
        stats = sb("stats", [P, CT, 6], f32)
        moments = sb("moments", [P, CT, 2], f32)
        rstd = sb("rstd", [P, CT], f32)
        var = sb("var", [P, CT], f32)
        guess = sb("guess", [P, CT], i32)
        newton = sb("newton", [P, CT], f32)
        w_sum = sb("w_sum", [P, 1], f32)
        w_mean = sb("w_mean", [P, 2, 1], f32)
        w_thr = sb("w_thr", [P, 2], f32)
        out_scale = sb("out_scale", [P, 2], f32)

        with ExitStack() as st:
            sb("before", [P, 4 * G * T - KF * D], f32, st)
            w_nat = sb("w_nat", [P, 2, KF, D], f32, st)
        with ExitStack() as st:
            sb("before2", [P, 4 * G * T], f32, st)
            wq_n = sb("wq_n", [P, KD, D], f32, st)
            wkv_n = sb("wkv_n", [2 * HD, D], f32, st)
        q_all = sb("q_all", [P, B, 2, G, T], f32r)

        with ExitStack() as st:
            sb("w_nat_rest", [P, KF * D], f32, st)
            with ExitStack() as st2:
                sb("before3", [P, KD * CW], f32, st2)
                wo_n = sb("wo_n", [P, KD, D], f32, st2)
            zT_hi = sb("zT_hi", [P, NCH, KD, CW], f32r, st)
            zT_lo = sb("zT_lo", [P, NCH, KD, CW], f32r, st)
            wq_hi = sb("wq_hi", [P, KD, D], f32r, st)
            wq_lo = sb("wq_lo", [P, KD, D], f32r, st)
            wkv_hi = sb("wkv_hi", [P, KD, 2 * HD], f32r, st)
            wkv_lo = sb("wkv_lo", [P, KD, 2 * HD], f32r, st)
            x_in = sb("x_in", [P, NCH, CT, D], f32, st)
            w_neg = sb("w_neg", [P, 2, D], f16, st)
            w_q16 = sb("w_q16", [P, 2, D], f16, st)
            v_st = sb("v_st", [HD, CW], f32, st)
        with ExitStack() as st:
            q_stack = sb("q_stack", [3 * HD + 2, B, NCH, HG, CW], f32r, st)
            prob = sb("prob", [P, 3, HG, CW], f32, st)
            den = sb("den", [P, NCH, CW], f32, st)
            raw = sb("raw", [P, NCH, CW], f32, st)
            peak_a = sb("peak_a", [P, NCH, HG, CT], f32, st)
            peak_b = sb("peak_b", [P, HG, CT], f32, st)
            peak_t = sb("peak_t", [HG * CT, NCH, 2, P], f32r, st)
        with ExitStack() as st:
            x2 = sb("x2", [P, NT, D], f32, st)
            z2 = sb("z2", [P, CT, D], f32, st)
            z2T_hi = sb("z2T_hi", [P, KD, CW], f16, st)
            z2T_lo = sb("z2T_lo", [P, KD, CW], f16, st)
            act_hi = sb("act_hi", [P, KF, CW], f16, st)
            act_lo = sb("act_lo", [P, KF, CW], f16, st)
            relu_s = sb("relu_s", [P, FB, CW], f32, st)
            sq_s = sb("sq_s", [P, FB, CW], f32, st)
            out_s = sb("out_s", [P, 2, D], f32, st)
        ps = ctx.enter_context(nc.psum_tensor("ps", [P, 8, CW], f32))

        wqkv_in, wo_in = sem("wqkv_in"), sem("wo_in")
        w_in = sem("w_in")
        bias_in = sem("bias_in")
        x_in_s = [sem(f"x_in_s{c}") for c in range(NCH)]
        const_ok = sem("const_ok")
        turned = sem("turned")
        mean_ok = sem("mean_ok")
        passed = sem("passed")
        ln_seq = sem("ln_seq")
        pool_seq = sem("pool_seq")
        wt_ready = sem("wt_ready")
        wt_hi = sem("wt_hi")
        wt_free = sem("wt_free")
        tern_sum = sem("tern_sum")
        tern_tot = sem("tern_tot")
        tern_thr = sem("tern_thr")
        tern_neg = sem("tern_neg")
        tern_q = sem("tern_q")
        tern_t = sem("tern_t")
        tern_done = sem("tern_done")
        z_ready = sem("z_ready")
        xt_ready = sem("xt_ready")
        xt_hi = sem("xt_hi")
        xt_free = sem("xt_free")
        pj_ready = sem("pj_ready")
        pj_hi = sem("pj_hi")
        pj_free = sem("pj_free")
        vt_ready = sem("vt_ready")
        vt_done = sem("vt_done")
        q_in = [[sem(f"q_in{b}_{c}") for c in range(NCH)] for b in range(B)]
        peak_ready = sem("peak_ready")
        peak_free = sem("peak_free")
        peaks_all = sem("peaks_all")
        peak_in = [sem(f"peak_in{c}") for c in range(NCH)]
        score_ready = sem("score_ready")
        exp_done = sem("exp_done")
        mask_done = sem("mask_done")
        value_done = sem("value_done")
        acc_free = sem("acc_free")
        den_free = sem("den_free")
        inverted = sem("inverted")
        output_step = sem("output_step")
        wo_ready = sem("wo_ready")
        x2_ready = sem("x2_ready")
        x2_in = [sem(f"x2_in{i}") for i in range(B * NCH)]
        x2_bias = sem("x2_bias")
        z2_ready = sem("z2_ready")
        t2_ready = sem("t2_ready")
        t2_hi = sem("t2_hi")
        t2_free = sem("t2_free")
        fc_ready = sem("fc_ready")
        relu_ok = sem("relu_ok")
        sq_ok = sem("sq_ok")
        act_hi_ok = sem("act_hi_ok")
        act_ok = sem("act_ok")
        pr_ready = sem("pr_ready")
        out_ok = sem("out_ok")
        out_in = [sem("out_in0"), sem("out_in1")]

        TP, PJ, WT, VT = (0, 1), (2, 3), (4, 5), 6
        PK, SC, AC, DN = (0, 1), (2, 4), 6, 7
        ONE = 1
        CRED = 2
        OCRED = NOUT + 1
        PCRED = 3

        block = ctx.enter_context(nc.Block())

        @block.sync
        def _(sp):
            for m in out_in:
                sp.sem_inc(m, ONE)
            sp.dma_start(wq_n[:, :, :], Wq.rearrange("(t p) d -> p t d", p=P)).then_inc(wqkv_in, 16)
            sp.dma_start(wkv_n[0:HD, :], Wv).then_inc(wqkv_in, 16)
            sp.dma_start(wkv_n[HD:2 * HD, :], Wk).then_inc(wqkv_in, 16)
            sp.dma_start(x_in[:, 0, :, :], x_t[0, :, :, :]).then_inc(x_in_s[0], 16)
            sp.dma_start(w_nat[:, 0, :, :], w_fc.rearrange("(t p) d -> p t d", p=P)).then_inc(w_in, 16)
            sp.dma_start(wo_n[:, :, :], Wo.rearrange("(t p) d -> p t d", p=P)).then_inc(wo_in, 16)
            sp.dma_start(x_in[:, 1, :, :], x_t[1, :, :, :]).then_inc(x_in_s[1], 16)
            sp.dma_start(bias_q[:, :], bq.rearrange("(g p) -> p g", p=P), allow_slow_non_contiguous=True).then_inc(bias_in, 16)
            sp.dma_start(bias_kv[0:HD, :], bv.rearrange("(p o) -> p o", o=1)).then_inc(bias_in, 16)
            sp.dma_start(bias_kv[HD:2 * HD, :], bk.rearrange("(p o) -> p o", o=1)).then_inc(bias_in, 16)
            sp.dma_start(bo_all[:, :], bo.rearrange("(o d) -> o d", o=1).broadcast_to([P, D])).then_inc(bias_in, 16)
            sp.wait_ge(xt_ready, CT)
            sp.dma_start(x_in[:, 0, :, :], x_t[2, :, :, :]).then_inc(x_in_s[0], 16)
            sp.wait_ge(tern_sum, 1)
            for t in range(KD):
                sp.dma_start(w_nat[:, 1, :, t * P:(t + 1) * P],
                             w_proj[t * P:(t + 1) * P, :].rearrange("p (f q) -> p f q", q=P)).then_inc(w_in, 16)
            sp.wait_ge(xt_ready, 2 * CT)
            sp.dma_start(x_in[:, 1, :, :], x_t[3, :, :, :]).then_inc(x_in_s[1], 16)

            def query_rows(g, b, c):
                for h in range(HG):
                    for row, part in ((0, 0), (HD, 0), (2 * HD, 1)):
                        sp.dma_start(q_stack[row:row + HD, b, c, h, :].bitcast(f32),
                                     q_all[h * HD:(h + 1) * HD, b, part, g, c * CW:(c + 1) * CW].bitcast(f32))\
                            .then_inc(q_in[b][c], 16)

            def peak_rows_in(n, b, c):
                sp.wait_ge(peak_free, CRED + NP * n + TURNS.index(("turn", c)) + 1)
                for part in range(2):
                    row = q_stack[3 * HD + part:3 * HD + part + 1, b, c, :, :].bitcast(f32)
                    sp.dma_start(row.rearrange("o h (i p) -> o (h i) p", p=P),
                                 peak_t[:, c, part, :].bitcast(f32)).then_inc(peak_in[c], 16)

            sp.wait_ge(pj_free, CRED + (G + 1) * 2 * B)
            sp.wait_ge(vt_done, ONE + NCH * B)
            sp.wait_ge(tern_done, ONE + 2 * KF)
            query_rows(0, 0, 0)
            query_rows(0, 0, 1)
            query_rows(0, 1, 0)
            peak_rows_in(0, 0, 0)
            peak_rows_in(0, 0, 1)

            def unit_loads(g, b, after):
                n = 2 * g + b
                sp.wait_ge(score_ready, ONE + NH * n)
                query_rows(g + b, 1 - b, 1)
                if after:
                    sp.wait_ge(score_ready, ONE + NH * n + 2 * CT)
                    query_rows(g + 1, b, 0)
                peak_rows_in(n + 1, 1 - b, 0)
                peak_rows_in(n + 1, 1 - b, 1)

            with sp.Fori(0, G - 1) as g:
                for b in range(B):
                    unit_loads(g, b, True)
            unit_loads(G - 1, 0, False)
            sp.wait_ge(score_ready, ONE + NH * B * G)
            for tl in range(0, NT, CT):
                sp.dma_start(x2[:, tl:tl + CT, :], x_t[tl // CT, :, :, :]).then_inc(x2_in[tl // CT], 16)

            with sp.Fori(0, B * NCH) as ch:
                for t in range(CT):
                    sp.wait_ge(out_ok, CRED + CT * ch + t + 1)
                    sp.dma_start(out_t[ch, :, t, :], out_s[:, t % 2, :]).then_inc(out_in[t % 2], 16)
            sp.wait_ge(out_in[0], ONE + 16 * NT // 2)
            sp.wait_ge(out_in[1], ONE + 16 * NT // 2)

        @block.gpsimd
        def _(pool):
            pool.sem_inc(output_step, OCRED)
            n_seq = [0]

            def link(ins):
                n_seq[0] += 1
                ins.then_inc(pool_seq, 1)
                pool.wait_ge(pool_seq, n_seq[0])

            for m in (ident, ident16, identb):
                link(nc.gpsimd.memset(m[:, :], 0.0))
                nc.gpsimd.affine_select(out=m[:, :], in_=m[:, :], compare_op=ALU.not_equal, fill=1.0, base=0,
                                        pattern=[[-1, P]], channel_multiplier=1).then_inc(const_ok, 1)
            nc.gpsimd.memset(ones[:, :], 1.0).then_inc(const_ok, 1)
            for m in (mask, mask_first):
                link(nc.gpsimd.memset(m[:, :], 0.0))
                ins = nc.gpsimd.affine_select(out=m[:, :], in_=m[:, :], compare_op=ALU.is_gt, fill=NEG, base=0,
                                              pattern=[[-1, P]], channel_multiplier=1)
                if m is mask_first:
                    link(ins)
                    ins = nc.gpsimd.memset(m[0:1, 0:1], 0.0)
                ins.then_inc(const_ok, 1)
            nc.gpsimd.memset(k_stack[3 * HD:3 * HD + 2, :, :].bitcast(f32), 1.0).then_inc(const_ok, 1)

            pool.wait_ge(const_ok, 7)
            for b in range(2):
                pool.wait_ge(tern_thr, b + 1)
                for i in range(KF):
                    pool.wait_ge(tern_q, ONE + KF * b + max(i - 1, 0))
                    nc.gpsimd.tensor_scalar(w_neg[:, i % 2, :], w_nat[:, b, i, :], w_thr[:, 1:2], None,
                                            ALU.is_lt).then_inc(tern_neg, 1)

            def unit(g, b, follows=True):
                n = 2 * g + b
                for ev in unit_order(False, follows):
                    if ev[0] == "score" and ev[2] == 1 and STEPS[ev[1]][4]:
                        pool.wait_ge(exp_done, CRED + NH * n + 2 * ev[1] + 2)
                        pool.sem_inc(passed, 1)
                        part = prob[:, ev[1] % 3, :, 0:P]
                        nc.gpsimd.affine_select(out=part, in_=part, compare_op=ALU.is_gt, fill=0.0, base=0,
                                                pattern=[[0, HG], [1, P]], channel_multiplier=-1).then_inc(mask_done, 1)
                    if ev[0] == "output":
                        output(g, b, n, *ev[1:])

            def output(g, b, n, part, c, back):
                u = NCH * (n - back) + c
                if back:
                    g, b = (g, 0) if b else (g - 1, 1)
                hi = q_all[:, b, 0, g, c * CW:(c + 1) * CW]
                lo = q_all[:, b, 1, g, c * CW:(c + 1) * CW]
                if part == 0:
                    pool.wait_ge(inverted, NINV * (u + 1))
                    pool.wait_ge(acc_free, ONE + u + 1)
                    nc.gpsimd.tensor_tensor(raw[:, c, :], raw[:, c, :], den[:, c, :], ALU.mult).then_inc(output_step, 1)
                elif part == 1:
                    pool.wait_ge(output_step, OCRED + NOUT * u + 1)
                    nc.gpsimd.tensor_copy(hi, raw[:, c, :]).then_inc(output_step, 1)
                else:
                    pool.wait_ge(output_step, OCRED + NOUT * u + 2)
                    nc.gpsimd.tensor_tensor(lo, raw[:, c, :], hi.bitcast(f32), ALU.subtract).then_inc(output_step, 1)

            unit(0, 0, False)
            with pool.Fori(0, G - 1) as g:
                unit(g, 1)
                unit(g + 1, 0)
            unit(G - 1, 1)
            for part in range(NOUT):
                output(G - 1, 1, B * G - 1, part, NCH - 1, 0)

            for tl in range(NT):
                pool.wait_ge(x2_in[tl // CT], 16)
                if tl == 0:
                    pool.wait_ge(bias_in, 64)
                nc.gpsimd.tensor_tensor(x2[:, tl, :], x2[:, tl, :], bo_all[:, :], ALU.add).then_inc(x2_bias, 1)

        @block.tensor
        def _(pe):
            pe.sem_inc(value_done, PCRED)
            for m in (vt_ready, score_ready, t2_ready):
                pe.sem_inc(m, ONE)
            pe.wait_ge(const_ok, 1)
            pe.wait_ge(wqkv_in, 48)
            for n in range(2 * KD + 1):
                if n == KD + 1:
                    pe.wait_ge(wo_in, 16)
                if n >= 2:
                    pe.wait_ge(wt_free, n - 1)
                bank = ps[:, WT[n % 2], :]
                if n == KD:
                    for k in range(KD):
                        ins = nc.tensor.transpose(bank[:, k * 2 * HD:(k + 1) * 2 * HD], wkv_n[:, k * P:(k + 1) * P],
                                                  ident[0:2 * HD, 0:2 * HD])
                else:
                    nat, k = (wq_n, n) if n < KD else (wo_n, n - KD - 1)
                    for t in range(KD):
                        ins = nc.tensor.transpose(bank[:, t * P:(t + 1) * P], nat[:, t, k * P:(k + 1) * P], ident[:, :])
                ins.then_inc(wt_ready, 1)

            def token_tile(b, c, t):
                s = 2 * b + c
                if t == 0:
                    pe.wait_ge(z_ready, s + 1)
                pe.wait_ge(xt_free, CT * s + t + 1)
                for k in range(KD):
                    ins = nc.tensor.transpose(ps[:, TP[t % 2], k * P:(k + 1) * P], x_in[:, c, t, k * P:(k + 1) * P],
                                              ident[:, :])
                ins.then_inc(xt_ready, 1)

            def project(b, c, m):
                s = 2 * b + c
                if m == 0:
                    pe.wait_ge(xt_free, CRED + CT * (s + 1))
                pe.wait_ge(pj_free, (G + 1) * s + m + 1)
                if m < G:
                    bank, wh, wl, cols = ps[:, PJ[m % 2], :], wq_hi, wq_lo, slice(m * P, (m + 1) * P)
                else:
                    bank, wh, wl, cols = ps[0:2 * HD, PJ[m % 2], :], wkv_hi, wkv_lo, slice(0, 2 * HD)
                terms = [(w, z, k) for w, z in ((wh, zT_hi), (wh, zT_lo), (wl, zT_hi)) for k in range(KD)]
                for i, (w, z, k) in enumerate(terms):
                    ins = nc.tensor.matmul(bank, w[:, k, cols], z[:, c, k, :], start=i == 0, stop=i == len(terms) - 1)
                ins.then_inc(pj_ready, 1)

            def values(b, c):
                s = 2 * b + c
                pe.wait_ge(pj_hi, (G + 1) * (s + 1))
                pe.wait_ge(vt_done, ONE + s)
                pe.sem_inc(passed, 1)
                for t in range(CT):
                    ins = nc.tensor.transpose(ps[:, VT, t * HD:(t + 1) * HD], v_st[:, t * P:(t + 1) * P], ident[0:HD, 0:HD])
                ins.then_inc(vt_ready, 1)

            def ternary(b, i):
                pe.wait_ge(tern_done, ONE + KF * b + max(i - 1, 0))
                pe.wait_ge(tern_q, ONE + KF * b + i + 1)
                bank = ps[:, WT[i % 2], :].bitcast(f16)
                for k in range(KD):
                    ins = nc.tensor.transpose(bank[:, k * P:(k + 1) * P], w_q16[:, i % 2, k * P:(k + 1) * P], ident16[:, :])
                ins.then_inc(tern_t, 1)

            pe.wait_ge(const_ok, 4)
            pe.wait_ge(wt_free, 2 * KD + 1)
            with pe.Fori(0, B) as b:
                for t in range(CT):
                    token_tile(b, 0, t)
                pe.wait_ge(tern_sum, b + 1)
                nc.tensor.matmul(ps[:, 7, 0:1], ones[:, :], w_sum[:, :], start=True, stop=True).then_inc(tern_tot, 1)
                for c in range(NCH):
                    for m in range(G + 1):
                        project(b, c, m)
                        if m:
                            ternary(b, (G + 1) * c + m - 1)
                        if c == 0 and m in (2, 3):
                            token_tile(b, 1, 2 * m - 4)
                            token_tile(b, 1, 2 * m - 3)
                    values(b, c)
                    ternary(b, (G + 1) * c + G)

            def peak(n, g, b, k, at):
                h0, nh, i, s0, w, diagonal = PEAKS[k]
                c, r = divmod(i, CT)
                if k == 0 or k == NPA:
                    pe.wait_ge(q_in[b][c], 16 * NQ * (g + 1))
                pe.wait_ge(peak_free, NP * n + at + 1)
                bank = ps[:, PK[at % 2], 0:nh * w].rearrange("p (h w) -> p h w", h=nh)
                for h in range(nh):
                    ins = nc.tensor.matmul(bank[:, h, :], q_stack[0:3 * HD, b, c, h0 + h, r * P:(r + 1) * P],
                                           k_stack[0:3 * HD, b, s0:s0 + w], start=h == 0, stop=not diagonal,
                                           skip_group_check=True)
                if diagonal:
                    m = (mask if i else mask_first)[:, :]
                    ins = nc.tensor.matmul(bank[:, :, w - P:w], identb[:, :], m.unsqueeze(1).broadcast_to([P, nh, P]),
                                           start=False, stop=True, skip_group_check=True)
                ins.then_inc(peak_ready, 1)

            def turn(n, c, at):
                if c == 0:
                    pe.wait_ge(peak_free, CRED + NP * n + NPA)
                else:
                    pe.wait_ge(peaks_all, n + 1)
                pe.wait_ge(peak_free, NP * n + at + 1)
                nc.tensor.transpose(ps[0:HG * CT, PK[at % 2], 0:P], peak_a[:, c, :, :].rearrange("p h i -> p (h i)"),
                                    ident[:, :]).then_inc(peak_ready, 1)

            def unit(g, b, with_peaks):
                n = 2 * g + b
                diag = 0
                for ev in unit_order(with_peaks):
                    if ev[0] == "score":
                        c, j, t0, w, _ = STEPS[ev[1]]
                        if j == 0 and ev[2] == 0:
                            pe.wait_ge(peak_in[c], 32 * (n + 1))
                        hs = 2 * ev[1] + ev[2]
                        pe.wait_ge(exp_done, NH * n + hs + 1)
                        for h in range(2):
                            ins = nc.tensor.matmul(ps[:, SC[hs % 2] + h, 0:w], k_stack[:, b, j * P:(j + 1) * P],
                                                   q_stack[:, b, c, 2 * ev[2] + h, t0 - c * CW:t0 - c * CW + w], start=True, stop=True)
                        ins.then_inc(score_ready, 1)
                    elif ev[0] == "peak":
                        peak(n + 1, g + b, 1 - b, ev[1], ev[2])
                    elif ev[0] == "turn":
                        turn(n + 1, ev[1], ev[2])
                    elif ev[0] == "value":
                        c, j, t0, w, diagonal = STEPS[ev[1]]
                        last = j == CT * (c + 1) - 1
                        if diagonal:
                            diag += 1
                            pe.wait_ge(mask_done, ND * n + diag)
                        else:
                            pe.wait_ge(exp_done, CRED + NH * n + 2 * ev[1] + 2)
                        if j == 0:
                            pe.wait_ge(acc_free, ONE + 2 * n + c)
                            pe.wait_ge(den_free, ONE + 2 * n + c)
                        cols = slice(t0 - c * CW, t0 - c * CW + w)
                        for h in range(HG):
                            nc.tensor.matmul(ps[h * HD:(h + 1) * HD, AC, cols], v_nat[:, b, j, :],
                                             prob[:, ev[1] % 3, h, 0:w], start=j == 0, stop=last)
                        for h in range(HG):
                            ins = nc.tensor.matmul(ps[h * HD:(h + 1) * HD, DN, cols], ones[:, 0:HD],
                                                   prob[:, ev[1] % 3, h, 0:w], start=j == 0, stop=last)
                        ins.then_inc(value_done, 1)

            pe.wait_ge(const_ok, 7)
            pe.wait_ge(vt_done, ONE + NCH * B)
            pe.wait_ge(tern_done, ONE + 2 * KF)
            pe.wait_ge(pj_free, CRED + (G + 1) * NCH * B)
            for at, (kind, a) in enumerate(TURNS):
                if kind == "peak":
                    peak(0, 0, 0, a, at)
                else:
                    turn(0, a, at)
            with pe.Fori(0, G - 1) as g:
                for b in range(B):
                    unit(g, b, True)
            unit(G - 1, 0, True)
            unit(G - 1, 1, False)

            for tl in range(NT):
                b, i = tl // TB, tl % TB
                if tl == 0:
                    pe.wait_ge(output_step, OCRED + NOUT * NCH * B * G)
                    pe.wait_ge(acc_free, ONE + NCH * B * G)
                    pe.wait_ge(den_free, ONE + NCH * B * G)
                if tl >= 2:
                    pe.wait_ge(x2_ready, tl - 1)
                terms = [(o, w, g) for o, w in ((0, wo_hi), (0, wo_lo), (1, wo_hi)) for g in range(G)]
                for n, (o, w, g) in enumerate(terms):
                    ins = nc.tensor.matmul(ps[:, 6 + tl % 2, :], q_all[:, b, o, g, i * P:(i + 1) * P], w[:, g, :],
                                           start=n == 0, stop=n == len(terms) - 1)
                ins.then_inc(wo_ready, 1)

            def token_tiles2(ch):
                pe.wait_ge(z2_ready, ch + 1)
                for t in range(CT):
                    pe.wait_ge(t2_free, CT * ch + t + 1)
                    for k in range(KD):
                        ins = nc.tensor.transpose(ps[:, TP[t % 2], k * P:(k + 1) * P], z2[:, t, k * P:(k + 1) * P], ident[:, :])
                    ins.then_inc(t2_ready, 1)

            def fc(ch):
                pe.wait_ge(t2_free, CRED + CT * (ch + 1))
                for f in range(KF):
                    pe.wait_ge(sq_ok, KF * ch + f + 1)
                    n = 0
                    for z in (z2T_hi, z2T_lo):
                        for k in range(KD):
                            ins = nc.tensor.matmul(ps[:, 2 + f % FB, :], w_T[:, 0, f, k * P:(k + 1) * P], z[:, k, :],
                                                   start=n == 0, stop=n == 2 * KD - 1)
                            n += 1
                    ins.then_inc(fc_ready, 1)

            def proj(ch):
                for t in range(CT):
                    pe.wait_ge(out_ok, CT * ch + t + 1)
                    for f in range(KF):
                        if t == 0:
                            pe.wait_ge(act_ok, ONE + KF * ch + f + 1)
                        for n, a in enumerate((act_hi, act_lo)):
                            ins = nc.tensor.matmul(ps[:, 6 + t % 2, :], a[:, f, t * P:(t + 1) * P], w_T[:, 1, f, :],
                                                   start=f == 0 and n == 0, stop=f == KF - 1 and n == 1)
                    ins.then_inc(pr_ready, 1)

            pe.wait_ge(peak_free, CRED + NP * B * G)
            pe.wait_ge(exp_done, CRED + NH * B * G)
            pe.wait_ge(mean_ok, B + 2)
            pe.wait_ge(x2_ready, NT)
            token_tiles2(0)
            with pe.Fori(0, B * NCH - 1) as ch:
                fc(ch)
                token_tiles2(ch + 1)
                proj(ch)
            fc(B * NCH - 1)
            proj(B * NCH - 1)

        @block.scalar
        def _(act):
            act.sem_inc(exp_done, CRED)
            for m in (vt_done, tern_done, acc_free):
                act.sem_inc(m, ONE)

            def copy(out_ap, in_ap):
                return nc.scalar.activation(out_ap, in_ap, ACT.Copy)

            for n in range(2 * KD + 1):
                act.wait_ge(wt_ready, n + 1)
                if n == KD:
                    copy(wkv_hi[:, :, :].rearrange("p k m -> p (k m)"), ps[:, WT[n % 2], 0:KD * 2 * HD]).then_inc(wt_hi, 1)
                else:
                    dst = wq_hi[:, n, :] if n < KD else wo_hi[:, n - KD - 1, :]
                    copy(dst, ps[:, WT[n % 2], :]).then_inc(wt_hi, 1)
            act.wait_ge(bias_in, 64)

            def token_tile(b, c, t):
                act.wait_ge(xt_ready, CT * (2 * b + c) + t + 1)
                copy(zT_hi[:, c, :, t * P:(t + 1) * P],
                     ps[:, TP[t % 2], :].rearrange("p (k t) -> p k t", k=KD)).then_inc(xt_hi, 1)

            def query(b, c, m):
                act.wait_ge(pj_ready, (G + 1) * (2 * b + c) + m + 1)
                act.sem_inc(passed, 1)
                nc.scalar.activation(q_all[:, b, 0, m, c * CW:(c + 1) * CW], ps[:, PJ[m % 2], :], ACT.Identity,
                                     bias=bias_q[:, m:m + 1]).then_inc(pj_hi, 1)

            def key_value(b, c):
                s = 2 * b + c
                act.wait_ge(pj_ready, (G + 1) * (s + 1))
                act.wait_ge(vt_ready, ONE + s)
                act.sem_inc(passed, 1)
                bank, cols = ps[:, PJ[G % 2], :], slice(c * CW, (c + 1) * CW)
                nc.scalar.activation(v_st[:, :], bank[0:HD, :], ACT.Identity, bias=bias_kv[0:HD, 0:1])
                for row in (2 * HD, 0):
                    ins = nc.scalar.activation(k_stack[row:row + HD, b, cols], bank[HD:2 * HD, :], ACT.Identity,
                                               bias=bias_kv[HD:2 * HD, 0:1])
                ins.then_inc(pj_hi, 1)

            def ternary(b, i):
                act.wait_ge(tern_t, KF * b + i + 1)
                act.sem_inc(passed, 1)
                copy(w_T[:, b, i, :], ps[:, WT[i % 2], :].bitcast(f16)[:, 0:D]).then_inc(tern_done, 1)

            with act.Fori(0, B) as b:
                act.wait_ge(w_in, 16 + 64 * b)
                act.sem_inc(passed, 1)
                nc.scalar.activation(w_T[:, b, :, :], w_nat[:, b, :, :], ACT.Abs, accum_out=w_sum[:, :]).then_inc(tern_sum, 1)
                for t in range(CT):
                    token_tile(b, 0, t)
                for c in range(NCH):
                    for m in range(G + 1):
                        if m < G:
                            query(b, c, m)
                        else:
                            key_value(b, c)
                        if m:
                            ternary(b, (G + 1) * c + m - 1)
                        if c == 0 and m in (2, 3):
                            token_tile(b, 1, 2 * m - 4)
                            token_tile(b, 1, 2 * m - 3)
                    act.wait_ge(vt_ready, ONE + 2 * b + c + 1)
                    act.sem_inc(passed, 1)
                    copy(v_nat[:, b, CT * c:CT * (c + 1), :],
                         ps[:, VT, 0:CT * HD].rearrange("p (t d) -> p t d", t=CT)).then_inc(vt_done, 1)
                    ternary(b, (G + 1) * c + G)

            def unit(g, b, with_peaks):
                n = 2 * g + b
                for ev in unit_order(with_peaks):
                    if ev[0] == "score":
                        w, hs = STEPS[ev[1]][3], 2 * ev[1] + ev[2]
                        if ev[2] == 0:
                            act.wait_ge(value_done, NS * n + ev[1] + 1)
                        act.wait_ge(score_ready, ONE + NH * n + hs + 1)
                        nc.scalar.activation(prob[:, ev[1] % 3, 2 * ev[2]:2 * ev[2] + 2, 0:w],
                                             ps[:, SC[hs % 2]:SC[hs % 2] + 2, 0:w], ACT.Exp, scale=SCALE).then_inc(exp_done, 1)
                    elif ev[0] == "sums":
                        u = NCH * n + ev[1]
                        act.wait_ge(output_step, OCRED + NOUT * (u - 1))
                        act.wait_ge(value_done, PCRED + NS * n + (CT if ev[1] == 0 else NS))
                        copy(raw[:, ev[1], :], ps[:, AC, :]).then_inc(acc_free, 1)

            with act.Fori(0, G - 1) as g:
                for b in range(B):
                    unit(g, b, True)
            unit(G - 1, 0, True)
            unit(G - 1, 1, False)

            def tokens2(ch):
                for t in range(CT):
                    act.wait_ge(t2_ready, ONE + CT * ch + t + 1)
                    copy(z2T_hi[:, :, t * P:(t + 1) * P],
                         ps[:, TP[t % 2], :].rearrange("p (k t) -> p k t", k=KD)).then_inc(t2_hi, 1)

            def fc(ch):
                def hi(f):
                    act.wait_ge(sq_ok, FB + KF * ch + f + 1)
                    copy(act_hi[:, f, :], sq_s[:, f % FB, :]).then_inc(act_hi_ok, 1)

                for f in range(KF):
                    act.wait_ge(fc_ready, KF * ch + f + 1)
                    act.wait_ge(sq_ok, KF * ch + f + 1)
                    nc.scalar.activation(relu_s[:, f % FB, :], ps[:, 2 + f % FB, :], ACT.Relu, scale=0.25).then_inc(relu_ok, 1)
                    if f:
                        hi(f - 1)
                hi(KF - 1)

            tokens2(0)
            with act.Fori(0, B * NCH - 1) as ch:
                fc(ch)
                tokens2(ch + 1)
            fc(B * NCH - 1)

        @block.vector
        def _(dve):
            for m in (xt_free, pj_free, peak_free, t2_free, out_ok):
                dve.sem_inc(m, CRED)
            dve.sem_inc(sq_ok, FB)
            for m in (den_free, act_ok, tern_q):
                dve.sem_inc(m, ONE)

            def minus(out_ap, in_ap, hi_ap):
                return nc.vector.tensor_tensor(out_ap, in_ap, hi_ap, ALU.subtract)

            def layer_norm(src, dst, base):
                for t in range(CT):
                    ins = nc.vector.bn_stats(stats[:, t, :], src(t))
                ins.then_inc(ln_seq, 1)
                dve.wait_ge(ln_seq, base + 1)
                dve.sem_inc(passed, 1)
                for t in range(CT):
                    ins = nc.vector.bn_aggr(moments[:, t, :], stats[:, t, :])
                ins.then_inc(ln_seq, 1)
                dve.wait_ge(ln_seq, base + 2)
                at = [base + 2]

                def step(ins):
                    at[0] += 1
                    ins.then_inc(ln_seq, 1)
                    dve.wait_ge(ln_seq, at[0])

                step(nc.vector.tensor_scalar(var[:, :], moments[:, :, 1], EPS, None, ALU.add))
                step(nc.vector.tensor_scalar(guess[:, :], var[:, :].bitcast(i32), 1, None, ALU.logical_shift_right))
                step(nc.vector.tensor_scalar(rstd[:, :].bitcast(i32), guess[:, :], -1.0, float(0x5F3759DF),
                                             ALU.mult, ALU.add))
                for _ in range(NEWTON):
                    step(nc.vector.tensor_tensor(newton[:, :], rstd[:, :], rstd[:, :], ALU.mult))
                    step(nc.vector.scalar_tensor_tensor(newton[:, :], newton[:, :], -0.5, var[:, :], ALU.mult, ALU.mult))
                    step(nc.vector.scalar_tensor_tensor(rstd[:, :], newton[:, :], 1.5, rstd[:, :], ALU.add, ALU.mult))
                for t in range(CT):
                    ins = nc.vector.tensor_scalar(dst(t), src(t), moments[:, t, 0:1], rstd[:, t:t + 1],
                                                  ALU.subtract, ALU.mult)
                return ins

            def norm1(b, c):
                dve.wait_ge(x_in_s[c], 16 * (b + 1))
                layer_norm(lambda t: x_in[:, c, t, :], lambda t: x_in[:, c, t, :], LN * (2 * b + c)).then_inc(z_ready, 1)

            for n in range(2 * KD + 1):
                dve.wait_ge(wt_hi, n + 1)
                if n == KD:
                    minus(wkv_lo[:, :, :].rearrange("p k m -> p (k m)"), ps[:, WT[n % 2], 0:KD * 2 * HD],
                          wkv_hi[:, :, :].rearrange("p k m -> p (k m)").bitcast(f32)).then_inc(wt_free, 1)
                else:
                    hi, lo, k = (wq_hi, wq_lo, n) if n < KD else (wo_hi, wo_lo, n - KD - 1)
                    minus(lo[:, k, :], ps[:, WT[n % 2], :], hi[:, k, :].bitcast(f32)).then_inc(wt_free, 1)
            dve.wait_ge(bias_in, 64)

            def token_tile(b, c, t):
                dve.wait_ge(xt_hi, CT * (2 * b + c) + t + 1)
                cols = slice(t * P, (t + 1) * P)
                minus(zT_lo[:, c, :, cols], ps[:, TP[t % 2], :].rearrange("p (k t) -> p k t", k=KD),
                      zT_hi[:, c, :, cols].bitcast(f32)).then_inc(xt_free, 1)

            def query(b, c, m):
                cols = slice(c * CW, (c + 1) * CW)
                dve.wait_ge(pj_hi, (G + 1) * (2 * b + c) + m + 1)
                nc.vector.scalar_tensor_tensor(q_all[:, b, 1, m, cols], ps[:, PJ[m % 2], :], bias_q[:, m:m + 1],
                                               q_all[:, b, 0, m, cols].bitcast(f32), ALU.add,
                                               ALU.subtract).then_inc(pj_free, 1)

            def keys(b, c):
                cols = slice(c * CW, (c + 1) * CW)
                dve.wait_ge(pj_hi, (G + 1) * (2 * b + c + 1))
                nc.vector.scalar_tensor_tensor(k_stack[HD:2 * HD, b, cols], ps[HD:2 * HD, PJ[G % 2], :],
                                               bias_kv[HD:2 * HD, 0:1], k_stack[0:HD, b, cols].bitcast(f32),
                                               ALU.add, ALU.subtract).then_inc(pj_free, 1)

            def ternary(b, i):
                dve.wait_ge(tern_neg, KF * b + i + 1)
                if i >= 2:
                    dve.wait_ge(tern_t, KF * b + i - 1)
                nc.vector.scalar_tensor_tensor(w_q16[:, i % 2, :], w_nat[:, b, i, :], w_thr[:, 0:1], w_neg[:, i % 2, :],
                                               ALU.is_gt, ALU.subtract).then_inc(tern_q, 1)

            with dve.Fori(0, B) as b:
                norm1(b, 0)
                for t in range(CT):
                    token_tile(b, 0, t)
                dve.wait_ge(tern_tot, b + 1)
                nc.vector.tensor_scalar(w_mean[:, b, :], ps[:, 7, 0:1], 1.0 / (D * F), 1e-5,
                                        ALU.mult, ALU.max).then_inc(mean_ok, 1)
                dve.wait_ge(mean_ok, b + 1)
                nc.vector.tensor_scalar(w_thr[:, 0:1], w_mean[:, b, :], 0.7, None, ALU.mult)
                nc.vector.tensor_scalar(w_thr[:, 1:2], w_mean[:, b, :], -0.7, None, ALU.mult).then_inc(tern_thr, 1)
                for c in range(NCH):
                    for m in range(G + 1):
                        if m < G:
                            query(b, c, m)
                        else:
                            keys(b, c)
                        if c == 0 and m == 0:
                            dve.wait_ge(tern_thr, b + 1)
                        ternary(b, (G + 1) * c + m)
                        if c == 0 and m == 0:
                            norm1(b, 1)
                        if c == 0 and m in (2, 3):
                            token_tile(b, 1, 2 * m - 4)
                            token_tile(b, 1, 2 * m - 3)
            nc.vector.tensor_scalar(out_scale[:, 1:2], w_mean[:, 0, :], w_mean[:, 0, :], 16.0, ALU.mult,
                                    ALU.mult).then_inc(mean_ok, 1)
            dve.wait_ge(mean_ok, B + 1)
            nc.vector.tensor_tensor(out_scale[:, 0:1], out_scale[:, 1:2], w_mean[:, 1, :], ALU.mult).then_inc(mean_ok, 1)

            def peak(n, k, at):
                h0, nh, i, s0, w, _ = PEAKS[k]
                c, r = divmod(i, CT)
                dve.wait_ge(peak_ready, NP * n + at + 1)
                dst = peak_b[:, h0:h0 + nh, r:r + 1] if s0 else peak_a[:, c, h0:h0 + nh, r:r + 1]
                src = ps[:, PK[at % 2], 0:nh * w].rearrange("p (h w) -> p h w", h=nh)
                nc.vector.tensor_reduce(dst, src, AXX, ALU.max).then_inc(peak_free, 1)

            def turn(n, c, at):
                if c == 1:
                    dve.wait_ge(peak_free, CRED + NP * n + at)
                    nc.vector.tensor_tensor(peak_a[:, 1, :, :], peak_a[:, 1, :, :], peak_b[:, :, :],
                                            ALU.max).then_inc(peaks_all, 1)
                dve.wait_ge(peak_ready, NP * n + at + 1)
                src = ps[0:HG * CT, PK[at % 2], 0:P]
                nc.vector.tensor_scalar(peak_t[:, c, 0, :], src, -1.0, None, ALU.mult).then_inc(turned, 1)
                dve.wait_ge(turned, 2 * n + c + 1)
                nc.vector.scalar_tensor_tensor(peak_t[:, c, 1, :], src, -1.0, peak_t[:, c, 0, :].bitcast(f32), ALU.mult,
                                               ALU.subtract).then_inc(peak_free, 1)

            def unit(g, b, with_peaks, follows=True):
                n = 2 * g + b
                for ev in unit_order(with_peaks, follows):
                    if ev[0] == "peak":
                        peak(n + 1, ev[1], ev[2])
                    elif ev[0] == "turn":
                        dve.wait_ge(peak_in[ev[1]], 32 * (n + 1))
                        turn(n + 1, ev[1], ev[2])
                    elif ev[0] == "sums":
                        c = ev[1]
                        u = NCH * n + c
                        dve.wait_ge(output_step, OCRED + NOUT * (u - 1))
                        dve.wait_ge(value_done, PCRED + NS * n + (CT if c == 0 else NS))
                        nc.vector.tensor_scalar(den[:, c, :], ps[:, DN, :], 1e-18, None, ALU.max).then_inc(den_free, 1)
                    elif ev[0] == "invert":
                        invert(n, *ev[1:])

            def invert(n, part, c, back):
                cols = slice(part * CW // NINV, (part + 1) * CW // NINV)
                if part == 0:
                    dve.wait_ge(den_free, ONE + NCH * (n - back) + c + 1)
                nc.vector.reciprocal(den[:, c, cols], den[:, c, cols]).then_inc(inverted, 1)

            for at, (kind, a) in enumerate(TURNS):
                if kind == "peak":
                    peak(0, a, at)
                else:
                    turn(0, a, at)
            unit(0, 0, True, False)
            with dve.Fori(0, G - 1) as g:
                unit(g, 1, True)
                unit(g + 1, 0, True)
            unit(G - 1, 1, False)
            for part in range(NINV):
                invert(B * G - 1, part, NCH - 1, 0)

            for tl in range(NT):
                dve.wait_ge(wo_ready, tl + 1)
                dve.wait_ge(x2_bias, tl + 1)
                nc.vector.tensor_tensor(x2[:, tl, :], ps[:, 6 + tl % 2, :], x2[:, tl, :], ALU.add).then_inc(x2_ready, 1)

            def norm2(ch):
                dve.wait_ge(x2_ready, CT * (ch + 1))
                dve.wait_ge(t2_ready, ONE + CT * ch)
                layer_norm(lambda t: x2[:, CT * ch + t, :], lambda t: z2[:, t, :],
                           LN * B * NCH + LN * ch).then_inc(z2_ready, 1)

            def tokens2(ch):
                for t in range(CT):
                    dve.wait_ge(t2_hi, CT * ch + t + 1)
                    cols = slice(t * P, (t + 1) * P)
                    minus(z2T_lo[:, :, cols], ps[:, TP[t % 2], :].rearrange("p (k t) -> p k t", k=KD),
                          z2T_hi[:, :, cols]).then_inc(t2_free, 1)

            def fc(ch, following):
                def lo(f):
                    dve.wait_ge(act_hi_ok, KF * ch + f + 1)
                    minus(act_lo[:, f, :], sq_s[:, f % FB, :], act_hi[:, f, :]).then_inc(act_ok, 1)

                for f in range(KF):
                    dve.wait_ge(act_ok, ONE + KF * ch + max(f - FB + 1, 0))
                    dve.wait_ge(relu_ok, KF * ch + f + 1)
                    nc.vector.scalar_tensor_tensor(sq_s[:, f % FB, :], ps[:, 2 + f % FB, :], 0.25, relu_s[:, f % FB, :],
                                                   ALU.mult, ALU.mult).then_inc(sq_ok, 1)
                    if f:
                        lo(f - 1)
                    if f == KF // 2 and following:
                        norm2(ch + 1)
                lo(KF - 1)

            def outputs(ch):
                for t in range(CT):
                    dve.wait_ge(pr_ready, CT * ch + t + 1)
                    dve.wait_ge(out_in[t % 2], ONE + 16 * ((CT // 2) * ch + t // 2))
                    nc.vector.scalar_tensor_tensor(out_s[:, t % 2, :], ps[:, 6 + t % 2, :], out_scale[:, 0:1],
                                                   x2[:, CT * ch + t, :], ALU.mult, ALU.add).then_inc(out_ok, 1)

            norm2(0)
            tokens2(0)
            with dve.Fori(0, B * NCH - 1) as ch:
                fc(ch, True)
                tokens2(ch + 1)
                outputs(ch)
            fc(B * NCH - 1, False)
            outputs(B * NCH - 1)


_INS = ["L0_attn_q_input", "L0_attn_Wq", "L0_attn_bq", "L0_attn_Wk", "L0_attn_bk", "L0_attn_Wv", "L0_attn_bv",
        "L0_attn_Wo", "L0_attn_bo", "L0_ffn_w_fc", "L0_ffn_w_proj"]


def kernel(**inputs):
    import numpy as _np
    import concourse.bacc as _bacc
    from concourse import mybir as _mybir
    from concourse.bass_utils import run_bass_kernel_spmd as _run

    nc = _bacc.Bacc("TRN2", target_bir_lowering=False, num_devices=1)
    arrays, args = {}, []
    for name in _INS:
        a = _np.ascontiguousarray(inputs[name])
        arrays[name + "_dram"] = a
        args.append(nc.dram_tensor(name + "_dram", a.shape, _mybir.dt.from_np(a.dtype), kind="ExternalInput").ap())
    x = arrays["L0_attn_q_input_dram"]
    args.append(nc.dram_tensor("out_dram", x.shape, _mybir.dt.from_np(x.dtype), kind="ExternalOutput").ap())
    preln_layer(nc, *args)
    r = _run(nc, [arrays], core_ids=[0])
    return r.results[0]["out_dram"]
```

```python
import concourse.bass as bass
from concourse import mybir
from concourse.alu_op_type import AluOpType as ALU
from contextlib import ExitStack




def preln_layer(nc, x, Wq, bq, Wk, bk, Wv, bv, Wo, bo, w_fc, w_proj, out):
    f32, f32r = mybir.dt.float32, mybir.dt.float32r
    f16, bf16 = mybir.dt.float16, mybir.dt.bfloat16
    ACT = mybir.ActivationFunctionType
    AXX = mybir.AxisListType.X

    P = 128
    B, T, D = x.shape
    HD = Wk.shape[0]
    H = D // HD
    F = w_fc.shape[0]
    KD = D // P
    KF = F // P
    HG = P // HD
    G = H // HG
    CW = 512
    NCH = T // CW
    TB = T // P
    CT = CW // P
    NT = B * TB
    EPS = 1e-5
    SCALE = float(HD) ** -0.5
    NEG = -1e30
    AHEAD = 2
    START = -0.03
    PACE = 0.91
    NEWTON = 3
    LN = 5 + 3 * NEWTON
    FB = 4
    i32 = mybir.dt.int32
    assert B == 2 and NCH == 2 and D == CW and HG == 4

    x_t = x.rearrange("b (c t p) d -> (b c) p t d", p=P, t=CT)
    out_t = out.rearrange("b (c t p) d -> (b c) p t d", p=P, t=CT)

    PEAKS = []
    for i in range(TB):
        for s0 in range(0, P * (i + 1), CW):
            w = min(CW, P * (i + 1) - s0)
            nh = max(1, min(HG, CW // w))
            for h0 in range(0, HG, nh):
                PEAKS.append((h0, nh, i, s0, w, s0 + w == P * (i + 1)))
    NPA = sum(p[2] < CT for p in PEAKS)
    TURNS = [("peak", k) for k in range(len(PEAKS))] + [("turn", 1)]
    TURNS.insert(NPA + 3, ("turn", 0))
    NPK = 3
    LAST = 1 + -len(TURNS) % NPK
    NP = len(TURNS) - 1 + LAST
    PEAK_WORK = [PEAKS[a][1] * PEAKS[a][4] + P if kind == "peak" else P for kind, a in TURNS]
    assert NP % NPK == 0 and TURNS[-1] == ("turn", NCH - 1)
    STEPS = []
    for c in range(NCH):
        for j in range(CT * (c + 1)):
            t0 = max(c * CW, j * P)
            STEPS.append((c, j, t0, (c + 1) * CW - t0, j * P >= c * CW))
    NS = len(STEPS)
    NH = HG * NS
    ND = sum(s[4] for s in STEPS)
    NQ = 3 * HG
    NINV, NOUT = 4, 3
    OUTPUT_STEPS = [("invert", i) for i in range(NINV)] + [("output", i) for i in range(NOUT)]

    NM = G + 1
    BETWEEN = {0: [], 1: [("values", 0), ("norm", 0)], 2: [("tokens", 0), ("tokens", 1), ("norm", 1)],
               3: [("tokens", 2), ("tokens", 3), ("norm", 2)], 4: []}
    SUM_AT = {2: 0, NM + 1: 1}

    PIECES = [min(2 * KF, max(0, 5 * (n - 1) // 3)) for n in range(B * NCH * NM)]
    EARLY_AT = (B * NCH - 1) * NM - 1
    EARLY = 4

    def projection_order():
        early = 0
        for n in range(B * NCH * NM):
            s, m = divmod(n, NM)
            if n >= EARLY_AT:
                for _ in range(EARLY):
                    yield (*TURNS[early], early)
                    early += 1
            yield "project", s, m
            if n in SUM_AT:
                yield "sum", SUM_AT[n], 0
            if n:
                for i in range(PIECES[n - 1] if n > 1 else 0, PIECES[n]):
                    yield "piece", i, 0
                for i in range(PIECES[n - 2] if n > 2 else 0, PIECES[n - 1]):
                    yield "place", i, 0
            for what, a in BETWEEN[m]:
                if what == "values":
                    yield what, s, a
                if what == "norm" and s + 2 < B * NCH:
                    yield what, s + 2, a
                if what == "tokens" and s + 1 < B * NCH:
                    yield what, s + 1, a

    EARLY_PEAKS = EARLY * (B * NCH * NM - EARLY_AT)

    WO_TERMS = 3 * G
    WO_EARLY = 3
    WO_FROM = 1

    def unit_order(first=False, last=False):
        order, todo, finish = [], [] if last else list(range(len(TURNS))), []
        whole, done, sent = float(sum(s[3] for s in STEPS)), 0.0, 0.0

        def peaks():
            nonlocal sent
            while todo and (len(todo) > 1 or done / whole > 0.97):
                if len(todo) > 1 and sent / sum(PEAK_WORK) > START + done / whole / PACE:
                    break
                m = todo.pop(0)
                order.append((*TURNS[m], m))
                sent += PEAK_WORK[m]

        def value(n, part, back):
            nonlocal done
            order.append(("value", n, part, back))
            done += 0.2 * STEPS[n][3]
            if part == 1 and (n == NS - 1 or STEPS[n + 1][0] != STEPS[n][0]):
                order.append(("sums", STEPS[n][0], back))
                finish.extend((kind, i, STEPS[n][0], back) for kind, i in OUTPUT_STEPS)
            peaks()

        for n, s in enumerate(STEPS):
            for half in range(2):
                order.append(("score", n, half))
                done += 0.3 * s[3]
                if finish and (finish[0][0] == "invert" or half):
                    order.append(finish.pop(0))
                peaks()
                if n >= AHEAD:
                    value(n - AHEAD, half, 0)
                elif not first:
                    value(NS - AHEAD + n, half, 1)
        done = whole
        peaks()
        if last:
            for n in range(NS - AHEAD, NS):
                for part in range(2):
                    value(n, part, 0)
            order += finish
            filled, k = [], 0
            for ev in order:
                filled.append(ev)
                if ev[0] in ("score", "value") and ev[1] >= WO_FROM and k < WO_EARLY * WO_TERMS:
                    filled.append(("project_out", k))
                    k += 1
            assert k == WO_EARLY * WO_TERMS
            order = filled
        assert not todo and (last or not finish)
        return order

    NORM_AT, TOKENS_AT = CT + 1, NT - CT
    FFN_OUT = [("out", 0), ("out", 1), ("tokens", 0), ("tokens", 1), ("out", 2), ("tokens", 2), ("tokens", 3), ("out", 3)]

    ctx = ExitStack()
    with ctx:
        def sb(name, shape, dt, stack=ctx):
            return stack.enter_context(nc.sbuf_tensor(name, shape, dt))

        def sem(name):
            return ctx.enter_context(nc.semaphore(name))

        k_stack = sb("k_stack", [3 * HD + 2, B, T], f32r)
        v_nat = sb("v_nat", [P, B, TB, HD], f32)
        wo_hi = sb("wo_hi", [P, KD, D], f32r)
        wo_lo = sb("wo_lo", [P, KD, D], f32r)
        w_T = sb("w_T", [P, 2, KF, D], f16)
        ident = sb("ident", [P, P], f32)
        ident16 = sb("ident16", [P, P], f16)
        identb = sb("identb", [P, P], bf16)
        mask_first = sb("mask_first", [P, P], bf16)
        mask = sb("mask", [P, P], bf16)
        ones = sb("ones", [P, P], f32)
        bias_q = sb("bias_q", [P, G], f32)
        bias_kv = sb("bias_kv", [2 * HD, 1], f32)
        stats = sb("stats", [P, CT, 6], f32)
        moments = sb("moments", [P, CT, 2], f32)
        rstd = sb("rstd", [P, CT], f32)
        var = sb("var", [P, CT], f32)
        guess = sb("guess", [P, CT], i32)
        newton = sb("newton", [P, CT], f32)
        w_sum = sb("w_sum", [P, 2], f32)
        w_mean = sb("w_mean", [P, 2, 1], f32)
        w_thr = sb("w_thr", [P, 2, 2], f32)
        out_scale = sb("out_scale", [P, 2], f32)

        peak_a = sb("peak_a", [P, NCH, HG, CT], f32)
        peak_b = sb("peak_b", [P, HG, CT], f32)
        peak_t = sb("peak_t", [HG * CT, NCH, 2, P], f32r)

        with ExitStack() as st:
            sb("before", [P, 4 * G * T - KF * D], f32, st)
            w_nat = sb("w_nat", [P, 2, KF, D], f32, st)
        with ExitStack() as st:
            sb("before2", [P, 4 * G * T], f32, st)
            wq_n = sb("wq_n", [P, KD, D], f32, st)
            wkv_n = sb("wkv_n", [2 * HD, D], f32, st)
        q_all = sb("q_all", [P, B, 2, G, T], f32r)

        with ExitStack() as st:
            sb("w_nat_rest", [P, KF * D], f32, st)
            with ExitStack() as st2:
                sb("before3", [P, KD * CW], f32, st2)
                wo_n = sb("wo_n", [P, KD, D], f32, st2)
            zT_hi = sb("zT_hi", [P, NCH, KD, CW], f32r, st)
            zT_lo = sb("zT_lo", [P, NCH, KD, CW], f32r, st)
            wq_hi = sb("wq_hi", [P, KD, D], f32r, st)
            wq_lo = sb("wq_lo", [P, KD, D], f32r, st)
            wkv_hi = sb("wkv_hi", [P, KD, 2 * HD], f32r, st)
            wkv_lo = sb("wkv_lo", [P, KD, 2 * HD], f32r, st)
            x_in = sb("x_in", [P, NCH, CT, D], f32, st)
            w_neg = sb("w_neg", [P, 2, D], f16, st)
            w_q16 = sb("w_q16", [P, 2, D], f16, st)
            v_st = sb("v_st", [HD, CW], f32, st)
        with ExitStack() as st:
            q_stack = sb("q_stack", [3 * HD + 2, B, NCH, HG, CW], f32r, st)
            prob = sb("prob", [P, 3, HG, CW], f32, st)
            den = sb("den", [P, NCH, CW], f32, st)
            raw = sb("raw", [P, NCH, CW], f32, st)
        with ExitStack() as st:
            x2 = sb("x2", [P, NT, D], f32, st)
            z2 = sb("z2", [P, CT, D], f32, st)
            z2T_hi = sb("z2T_hi", [P, KD, CW], f16, st)
            z2T_lo = sb("z2T_lo", [P, KD, CW], f16, st)
            act_hi = sb("act_hi", [P, KF, CW], f16, st)
            act_lo = sb("act_lo", [P, KF, CW], f16, st)
            bo_all = sb("bo_all", [P, D], f32, st)
            relu_s = sb("relu_s", [P, FB, CW], f32, st)
            sq_s = sb("sq_s", [P, FB, CW], f32, st)
            out_s = sb("out_s", [P, 2, D], f32, st)
        ps = ctx.enter_context(nc.psum_tensor("ps", [P, 8, CW], f32))

        wq_in, wkv_in, wo_in = sem("wq_in"), sem("wkv_in"), sem("wo_in")
        w_in = [sem("w_fc_in"), sem("w_proj_in")]
        bias_in, bo_in = sem("bias_in"), sem("bo_in")
        x_in_s = [sem(f"x_in_s{c}") for c in range(NCH)]
        const_ok = sem("const_ok")
        turned = sem("turned")
        mean_ok = sem("mean_ok")
        passed = sem("passed")
        ln_seq = sem("ln_seq")
        pool_seq = sem("pool_seq")
        wt_ready = sem("wt_ready")
        wt_hi = sem("wt_hi")
        wt_free = sem("wt_free")
        tern_sum = sem("tern_sum")
        tern_tot = sem("tern_tot")
        tern_thr = sem("tern_thr")
        tern_neg = sem("tern_neg")
        tern_q = sem("tern_q")
        tern_t = sem("tern_t")
        tern_done = sem("tern_done")
        z_ready = sem("z_ready")
        xt_ready = sem("xt_ready")
        xt_hi = sem("xt_hi")
        xt_free = sem("xt_free")
        pj_ready = sem("pj_ready")
        pj_hi = sem("pj_hi")
        pj_free = sem("pj_free")
        vt_ready = sem("vt_ready")
        vt_done = sem("vt_done")
        q_in = [[sem(f"q_in{b}_{c}") for c in range(NCH)] for b in range(B)]
        peak_ready = sem("peak_ready")
        peak_free = sem("peak_free")
        peaks_all = sem("peaks_all")
        peak_in = [sem(f"peak_in{c}") for c in range(NCH)]
        score_ready = sem("score_ready")
        exp_done = sem("exp_done")
        mask_done = sem("mask_done")
        value_done = sem("value_done")
        acc_free = sem("acc_free")
        den_free = sem("den_free")
        inverted = sem("inverted")
        output_step = sem("output_step")
        wo_ready = sem("wo_ready")
        x2_ready = sem("x2_ready")
        x2_in = [sem(f"x2_in{i}") for i in range(B * NCH)]
        x2_bias = sem("x2_bias")
        z2_ready = sem("z2_ready")
        t2_ready = sem("t2_ready")
        t2_hi = sem("t2_hi")
        t2_free = sem("t2_free")
        fc_ready = sem("fc_ready")
        relu_ok = sem("relu_ok")
        sq_ok = sem("sq_ok")
        act_hi_ok = sem("act_hi_ok")
        act_ok = sem("act_ok")
        pr_ready = sem("pr_ready")
        out_ok = sem("out_ok")
        out_in = [sem("out_in0"), sem("out_in1")]

        TP, PJ, WT, VT = (0, 1), (2, 3), (4, 5), 6
        WBANK = (4, 5, 2, 3, 6, 4, 5, 4, 5)
        T2, OT = (6, 7), (0, 1)
        PK, SC, AC, DN = (0, 1, 7), (2, 3, 4), 5, 6
        ONE = 1
        CRED = 2
        OCRED = NOUT + 1
        PCRED = 3
        BCRED = 3

        block = ctx.enter_context(nc.Block())

        @block.sync
        def _(sp):
            for m in out_in:
                sp.sem_inc(m, ONE)
            sp.dma_start(x_in[:, 0, :, :], x_t[0, :, :, :]).then_inc(x_in_s[0], 16)
            sp.dma_start(wq_n[:, :, :], Wq.rearrange("(t p) d -> p t d", p=P)).then_inc(wq_in, 16)
            sp.dma_start(wkv_n[0:HD, :], Wv).then_inc(wkv_in, 16)
            sp.dma_start(wkv_n[HD:2 * HD, :], Wk).then_inc(wkv_in, 16)
            sp.dma_start(wo_n[:, :, :], Wo.rearrange("(t p) d -> p t d", p=P)).then_inc(wo_in, 16)
            sp.dma_start(x_in[:, 1, :, :], x_t[1, :, :, :]).then_inc(x_in_s[1], 16)
            sp.dma_start(bias_kv[0:HD, :], bv.rearrange("(p o) -> p o", o=1)).then_inc(bias_in, 16)
            sp.dma_start(bias_kv[HD:2 * HD, :], bk.rearrange("(p o) -> p o", o=1)).then_inc(bias_in, 16)
            sp.dma_start(bias_q[:, :], bq.rearrange("(g p) -> p g", p=P), allow_slow_non_contiguous=True).then_inc(bias_in, 16)
            sp.dma_start(w_nat[:, 0, :, :], w_fc.rearrange("(t p) d -> p t d", p=P)).then_inc(w_in[0], 16)
            sp.wait_ge(wt_ready, KD + 1)
            for t in range(KD):
                sp.dma_start(w_nat[:, 1, :, t * P:(t + 1) * P],
                             w_proj[t * P:(t + 1) * P, :].rearrange("p (f q) -> p f q", q=P)).then_inc(w_in[1], 16)
            for c in range(NCH):
                sp.wait_ge(xt_ready, CT * (c + 1))
                sp.dma_start(x_in[:, c, :, :], x_t[NCH + c, :, :, :]).then_inc(x_in_s[c], 16)

            def query_rows(g, b, c):
                for h in range(HG):
                    for row, part in ((0, 0), (HD, 0), (2 * HD, 1)):
                        sp.dma_start(q_stack[row:row + HD, b, c, h, :].bitcast(f32),
                                     q_all[h * HD:(h + 1) * HD, b, part, g, c * CW:(c + 1) * CW].bitcast(f32))\
                            .then_inc(q_in[b][c], 16)

            def peak_rows_in(n, b, c):
                sp.wait_ge(peak_free, BCRED + NP * n + TURNS.index(("turn", c)) + 1)
                for part in range(2):
                    row = q_stack[3 * HD + part:3 * HD + part + 1, b, c, :, :].bitcast(f32)
                    sp.dma_start(row.rearrange("o h (i p) -> o (h i) p", p=P),
                                 peak_t[:, c, part, :].bitcast(f32)).then_inc(peak_in[c], 16)

            for c in range(NCH):
                sp.wait_ge(pj_free, CRED + NM * (c + 1))
                sp.wait_ge(tern_q, KF + CT * (c + 1))
                query_rows(0, 0, c)
            peak_rows_in(0, 0, 0)
            sp.wait_ge(pj_free, CRED + NM * B * NCH)
            sp.wait_ge(vt_done, NCH * B)
            query_rows(0, 1, 0)
            peak_rows_in(0, 0, 1)

            def unit_loads(g, b, after):
                n = 2 * g + b
                sp.wait_ge(score_ready, ONE + NH * n)
                query_rows(g + b, 1 - b, 1)
                if after:
                    sp.wait_ge(score_ready, ONE + NH * n + HG * CT)
                    query_rows(g + 1, b, 0)
                peak_rows_in(n + 1, 1 - b, 0)
                peak_rows_in(n + 1, 1 - b, 1)

            with sp.Fori(0, G - 1) as g:
                for b in range(B):
                    unit_loads(g, b, True)
            unit_loads(G - 1, 0, False)
            sp.wait_ge(score_ready, ONE + NH * (B * G - 1))
            sp.dma_start(bo_all[:, :], bo.rearrange("(o d) -> o d", o=1).broadcast_to([P, D])).then_inc(bo_in, 16)
            for tl in range(0, NT, CT):
                if tl == TB:
                    sp.wait_ge(score_ready, ONE + NH * B * G)
                sp.dma_start(x2[:, tl:tl + CT, :], x_t[tl // CT, :, :, :]).then_inc(x2_in[tl // CT], 16)

            with sp.Fori(0, B * NCH) as ch:
                for t in range(CT):
                    sp.wait_ge(out_ok, CRED + CT * ch + t + 1)
                    sp.dma_start(out_t[ch, :, t, :], out_s[:, t % 2, :]).then_inc(out_in[t % 2], 16)
            sp.wait_ge(out_in[0], ONE + 16 * NT // 2)
            sp.wait_ge(out_in[1], ONE + 16 * NT // 2)

        @block.gpsimd
        def _(pool):
            pool.sem_inc(output_step, OCRED)
            n_seq = [0]

            def link(ins):
                n_seq[0] += 1
                ins.then_inc(pool_seq, 1)
                pool.wait_ge(pool_seq, n_seq[0])

            for m in (ident, ident16, identb):
                link(nc.gpsimd.memset(m[:, :], 0.0))
                nc.gpsimd.affine_select(out=m[:, :], in_=m[:, :], compare_op=ALU.not_equal, fill=1.0, base=0,
                                        pattern=[[-1, P]], channel_multiplier=1).then_inc(const_ok, 1)
            nc.gpsimd.memset(ones[:, :], 1.0).then_inc(const_ok, 1)
            for m in (mask, mask_first):
                link(nc.gpsimd.memset(m[:, :], 0.0))
                ins = nc.gpsimd.affine_select(out=m[:, :], in_=m[:, :], compare_op=ALU.is_gt, fill=NEG, base=0,
                                              pattern=[[-1, P]], channel_multiplier=1)
                if m is mask_first:
                    link(ins)
                    ins = nc.gpsimd.memset(m[0:1, 0:1], 0.0)
                ins.then_inc(const_ok, 1)
            nc.gpsimd.memset(k_stack[3 * HD:3 * HD + 2, :, :].bitcast(f32), 1.0).then_inc(const_ok, 1)

            pool.wait_ge(const_ok, 7)
            for b in range(2):
                pool.wait_ge(tern_thr, b + 1)
                for i in range(KF):
                    if KF * b + i >= 2:
                        pool.wait_ge(tern_q, KF * b + i - 1)
                    nc.gpsimd.tensor_scalar(w_neg[:, i % 2, :], w_nat[:, b, i, :], w_thr[:, b, 1:2], None,
                                            ALU.is_lt).then_inc(tern_neg, 1)

            def unit(g, b, **ends):
                n = 2 * g + b
                for ev in unit_order(**ends):
                    if ev[0] == "score" and ev[2] == 1 and STEPS[ev[1]][4]:
                        pool.wait_ge(exp_done, BCRED + NH * n + HG * (ev[1] + 1))
                        pool.sem_inc(passed, 1)
                        part = prob[:, ev[1] % 3, :, 0:P]
                        nc.gpsimd.affine_select(out=part, in_=part, compare_op=ALU.is_gt, fill=0.0, base=0,
                                                pattern=[[0, HG], [1, P]], channel_multiplier=-1).then_inc(mask_done, 1)
                    if ev[0] == "output":
                        output(g, b, n, *ev[1:])

            def output(g, b, n, part, c, back):
                u = NCH * (n - back) + c
                if back:
                    g, b = (g, 0) if b else (g - 1, 1)
                hi = q_all[:, b, 0, g, c * CW:(c + 1) * CW]
                lo = q_all[:, b, 1, g, c * CW:(c + 1) * CW]
                if part == 0:
                    pool.wait_ge(inverted, NINV * (u + 1))
                    pool.wait_ge(acc_free, ONE + u + 1)
                    nc.gpsimd.tensor_tensor(raw[:, c, :], raw[:, c, :], den[:, c, :], ALU.mult).then_inc(output_step, 1)
                elif part == 1:
                    pool.wait_ge(output_step, OCRED + NOUT * u + 1)
                    nc.gpsimd.tensor_copy(hi, raw[:, c, :]).then_inc(output_step, 1)
                else:
                    pool.wait_ge(output_step, OCRED + NOUT * u + 2)
                    nc.gpsimd.tensor_tensor(lo, raw[:, c, :], hi.bitcast(f32), ALU.subtract).then_inc(output_step, 1)

            unit(0, 0, first=True)
            with pool.Fori(0, G - 1) as g:
                unit(g, 1)
                unit(g + 1, 0)
            unit(G - 1, 1, last=True)

        @block.tensor
        def _(pe):
            pe.sem_inc(value_done, PCRED)
            for m in (score_ready, t2_ready):
                pe.sem_inc(m, ONE)
            pe.wait_ge(const_ok, 1)

            def weight(n):
                if WBANK[n] in WBANK[:n]:
                    pe.wait_ge(wt_free, max(i for i in range(n) if WBANK[i] == WBANK[n]) + 1)
                bank = ps[:, WBANK[n], :]
                if n == KD:
                    for k in range(KD):
                        ins = nc.tensor.transpose(bank[:, k * 2 * HD:(k + 1) * 2 * HD], wkv_n[:, k * P:(k + 1) * P],
                                                  ident[0:2 * HD, 0:2 * HD])
                else:
                    nat, k = (wq_n, n) if n < KD else (wo_n, n - KD - 1)
                    for t in range(KD):
                        ins = nc.tensor.transpose(bank[:, t * P:(t + 1) * P], nat[:, t, k * P:(k + 1) * P], ident[:, :])
                ins.then_inc(wt_ready, 1)

            def token_tile(s, t):
                if t == 0:
                    pe.wait_ge(z_ready, s + 1)
                pe.wait_ge(xt_free, CT * s + t + 1)
                for k in range(KD):
                    ins = nc.tensor.transpose(ps[:, TP[t % 2], k * P:(k + 1) * P],
                                              x_in[:, s % NCH, t, k * P:(k + 1) * P], ident[:, :])
                ins.then_inc(xt_ready, 1)

            def project(s, m, early):
                if m == 0:
                    pe.wait_ge(xt_free, CRED + CT * (s + 1))
                n = NM * s + m
                pe.wait_ge(pj_free, n + 1)
                if m:
                    bank, wh, wl, cols = ps[:, PJ[n % 2], :], wq_hi, wq_lo, slice((m - 1) * P, m * P)
                else:
                    bank, wh, wl, cols = ps[0:2 * HD, PJ[n % 2], :], wkv_hi, wkv_lo, slice(0, 2 * HD)
                terms = [(w, z, k) for w, z in ((wh, zT_hi), (wh, zT_lo), (wl, zT_hi)) for k in range(KD)]
                for i, (w, z, k) in enumerate(terms):
                    if early and i % 3 == 2:
                        first_peaks(*early.pop(0))
                    ins = nc.tensor.matmul(bank, w[:, k, cols], z[:, s % NCH, k, :], start=i == 0, stop=i == len(terms) - 1)
                ins.then_inc(pj_ready, 1)

            def peak(n, g, b, k, at):
                h0, nh, i, s0, w, diagonal = PEAKS[k]
                c, r = divmod(i, CT)
                if k == 0 or k == NPA:
                    pe.wait_ge(q_in[b][c], 16 * NQ * (g + 1))
                pe.wait_ge(peak_free, NP * n + at + 1)
                bank = ps[:, PK[at % NPK], 0:nh * w].rearrange("p (h w) -> p h w", h=nh)
                for h in range(nh):
                    ins = nc.tensor.matmul(bank[:, h, :], q_stack[0:3 * HD, b, c, h0 + h, r * P:(r + 1) * P],
                                           k_stack[0:3 * HD, b, s0:s0 + w], start=h == 0, stop=not diagonal,
                                           skip_group_check=True)
                if diagonal:
                    m = (mask if i else mask_first)[:, :]
                    ins = nc.tensor.matmul(bank[:, :, w - P:w], identb[:, :], m.unsqueeze(1).broadcast_to([P, nh, P]),
                                           start=False, stop=True, skip_group_check=True)
                ins.then_inc(peak_ready, 1)

            def turn(n, c, at):
                if c == 0:
                    pe.wait_ge(peak_free, BCRED + NP * n + NPA)
                else:
                    pe.wait_ge(peaks_all, n + 1)
                pe.wait_ge(peak_free, NP * n + at + 1)
                nc.tensor.transpose(ps[0:HG * CT, PK[at % NPK], 0:P], peak_a[:, c, :, :].rearrange("p h i -> p (h i)"),
                                    ident[:, :]).then_inc(peak_ready, LAST if c == NCH - 1 else 1)

            def first_peaks(kind, a, at):
                if at == 0:
                    pe.wait_ge(xt_free, CRED + NT)
                    pe.wait_ge(mean_ok, B)
                if kind == "peak":
                    peak(0, 0, 0, a, at)
                else:
                    turn(0, a, at)

            def values(s):
                pe.wait_ge(pj_hi, NM * s + 1)
                if s:
                    pe.wait_ge(vt_done, s)
                for t in range(CT):
                    ins = nc.tensor.transpose(ps[:, VT, t * HD:(t + 1) * HD], v_st[:, t * P:(t + 1) * P], ident[0:HD, 0:HD])
                ins.then_inc(vt_ready, 1)

            def piece(i):
                if i == 0:
                    pe.wait_ge(wt_free, 2 * KD + 1)
                if i >= 2:
                    pe.wait_ge(tern_done, i - 1)
                pe.wait_ge(tern_q, i + 1)
                bank = ps[:, WT[i % 2], :].bitcast(f16)
                for k in range(KD):
                    ins = nc.tensor.transpose(bank[:, k * P:(k + 1) * P], w_q16[:, i % 2, k * P:(k + 1) * P], ident16[:, :])
                ins.then_inc(tern_t, 1)

            def total(b):
                pe.wait_ge(tern_sum, b + 1)
                nc.tensor.matmul(ps[:, 7, b:b + 1], ones[:, :], w_sum[:, b:b + 1], start=True, stop=True).then_inc(tern_tot, 1)

            pe.wait_ge(wq_in, 16)
            for n in range(KD):
                weight(n)
            pe.wait_ge(wkv_in, 32)
            weight(KD)
            for t in range(CT):
                token_tile(0, t)
            pe.wait_ge(wo_in, 16)
            for n in range(KD + 1, 2 * KD + 1):
                weight(n)
            pe.wait_ge(const_ok, 7)
            early = []
            for what, s, a in projection_order():
                if what in ("peak", "turn"):
                    early.append((what, s, a))
                elif what == "project":
                    project(s, a, early)
                elif what == "sum":
                    total(s)
                elif what == "values":
                    values(s)
                elif what == "tokens":
                    token_tile(s, a)
                elif what == "place":
                    piece(s)

            def value(b, n, step, part):
                c, j, t0, w, diagonal = STEPS[step]
                last = j == CT * (c + 1) - 1
                cols = slice(t0 - c * CW, t0 - c * CW + w)
                if part == 0:
                    if diagonal:
                        pe.wait_ge(mask_done, ND * n + sum(s[4] for s in STEPS[:step + 1]))
                    else:
                        pe.wait_ge(exp_done, BCRED + NH * n + HG * (step + 1))
                    if j == 0:
                        pe.wait_ge(acc_free, ONE + 2 * n + c)
                elif j == 0:
                    pe.wait_ge(den_free, ONE + 2 * n + c)
                for h in range(HG):
                    ins = nc.tensor.matmul(ps[h * HD:(h + 1) * HD, DN if part else AC, cols],
                                           ones[:, 0:HD] if part else v_nat[:, b, j, :],
                                           prob[:, step % 3, h, 0:w], start=j == 0, stop=last)
                if part:
                    ins.then_inc(value_done, 1)

            def project_out(tl, n):
                b, i = tl // TB, tl % TB
                if tl == 0 and n == 0:
                    pe.wait_ge(peak_free, BCRED + NP * B * G)
                if i % CT == 0 and n == 0:
                    pe.wait_ge(output_step, OCRED + NOUT * (NCH * (B * (G - 1) + b) + i // CT + 1))
                if tl >= 2 and n == 0:
                    pe.wait_ge(x2_ready, tl - 1)
                o, w = ((0, wo_hi), (0, wo_lo), (1, wo_hi))[n // G]
                ins = nc.tensor.matmul(ps[:, PK[tl % 2], :], q_all[:, b, o, n % G, i * P:(i + 1) * P], w[:, n % G, :],
                                       start=n == 0, stop=n == WO_TERMS - 1)
                if n == WO_TERMS - 1:
                    ins.then_inc(wo_ready, 1)

            def unit(g, b, **ends):
                n = 2 * g + b
                for ev in unit_order(**ends):
                    if ev[0] == "score":
                        c, j, t0, w, _ = STEPS[ev[1]]
                        if j == 0 and ev[2] == 0:
                            pe.wait_ge(peak_in[c], 32 * (n + 1))
                        for h in range(2 * ev[2], 2 * ev[2] + 2):
                            at = HG * ev[1] + h
                            pe.wait_ge(exp_done, NH * n + at + 1)
                            nc.tensor.matmul(ps[:, SC[at % 3], 0:w], k_stack[:, b, j * P:(j + 1) * P],
                                             q_stack[:, b, c, h, t0 - c * CW:t0 - c * CW + w], start=True,
                                             stop=True).then_inc(score_ready, 1)
                    elif ev[0] == "peak":
                        peak(n + 1, g + b, 1 - b, ev[1], ev[2])
                    elif ev[0] == "turn":
                        turn(n + 1, ev[1], ev[2])
                    elif ev[0] == "value":
                        _, step, part, back = ev
                        value(1 - b if back else b, n - back, step, part)
                    elif ev[0] == "project_out":
                        project_out(*divmod(ev[1], WO_TERMS))

            pe.wait_ge(vt_done, NCH * B)
            pe.wait_ge(pj_free, CRED + NM * NCH * B)
            for at in range(EARLY_PEAKS, len(TURNS)):
                first_peaks(*TURNS[at], at)
            unit(0, 0, first=True)
            with pe.Fori(0, G - 1) as g:
                unit(g, 1)
                unit(g + 1, 0)
            unit(G - 1, 1, last=True)

            def token_tile2(ch, t):
                if t == 0:
                    pe.wait_ge(z2_ready, ch + 1)
                pe.wait_ge(t2_free, CT * ch + t + 1)
                for k in range(KD):
                    ins = nc.tensor.transpose(ps[:, T2[t % 2], k * P:(k + 1) * P], z2[:, t, k * P:(k + 1) * P], ident[:, :])
                ins.then_inc(t2_ready, 1)

            for tl in range(WO_EARLY, NT):
                for n in range(WO_TERMS):
                    project_out(tl, n)
                if tl == TOKENS_AT:
                    pe.wait_ge(acc_free, ONE + NCH * B * G)
                    pe.wait_ge(den_free, ONE + NCH * B * G)
                if tl >= TOKENS_AT:
                    token_tile2(0, tl - TOKENS_AT)

            def fc(ch):
                pe.wait_ge(t2_free, CRED + CT * (ch + 1))
                for f in range(KF):
                    pe.wait_ge(sq_ok, KF * ch + f + 1)
                    n = 0
                    for z in (z2T_hi, z2T_lo):
                        for k in range(KD):
                            ins = nc.tensor.matmul(ps[:, 2 + f % FB, :], w_T[:, 0, f, k * P:(k + 1) * P], z[:, k, :],
                                                   start=n == 0, stop=n == 2 * KD - 1)
                            n += 1
                    ins.then_inc(fc_ready, 1)

            def proj(ch, t):
                pe.wait_ge(out_ok, CT * ch + t + 1)
                for f in range(KF):
                    if t == 0:
                        pe.wait_ge(act_ok, ONE + KF * ch + f + 1)
                    for n, a in enumerate((act_hi, act_lo)):
                        ins = nc.tensor.matmul(ps[:, OT[t % 2], :], a[:, f, t * P:(t + 1) * P], w_T[:, 1, f, :],
                                               start=f == 0 and n == 0, stop=f == KF - 1 and n == 1)
                ins.then_inc(pr_ready, 1)

            def outputs(ch, following):
                for what, t in FFN_OUT:
                    if what == "out":
                        proj(ch, t)
                    elif following:
                        token_tile2(ch + 1, t)

            pe.wait_ge(exp_done, BCRED + NH * B * G)
            pe.wait_ge(mean_ok, B + 2)
            pe.wait_ge(x2_ready, NT)
            with pe.Fori(0, B * NCH - 1) as ch:
                fc(ch)
                outputs(ch, True)
            fc(B * NCH - 1)
            outputs(B * NCH - 1, False)

        @block.scalar
        def _(act):
            act.sem_inc(exp_done, BCRED)
            for m in (den_free, acc_free):
                act.sem_inc(m, ONE)

            def copy(out_ap, in_ap):
                return nc.scalar.activation(out_ap, in_ap, ACT.Copy)

            def weight(n):
                act.wait_ge(wt_ready, n + 1)
                if n == KD:
                    copy(wkv_hi[:, :, :].rearrange("p k m -> p (k m)"), ps[:, WBANK[n], 0:KD * 2 * HD]).then_inc(wt_hi, 1)
                else:
                    dst = wq_hi[:, n, :] if n < KD else wo_hi[:, n - KD - 1, :]
                    copy(dst, ps[:, WBANK[n], :]).then_inc(wt_hi, 1)

            def token_tile(s, t):
                act.wait_ge(xt_ready, CT * s + t + 1)
                copy(zT_hi[:, s % NCH, :, t * P:(t + 1) * P],
                     ps[:, TP[t % 2], :].rearrange("p (k t) -> p k t", k=KD)).then_inc(xt_hi, 1)

            def project(s, m):
                n = NM * s + m
                b, cols, bank = s // NCH, slice(s % NCH * CW, (s % NCH + 1) * CW), ps[:, PJ[n % 2], :]
                act.wait_ge(pj_ready, n + 1)
                if m:
                    nc.scalar.activation(q_all[:, b, 0, m - 1, cols], bank, ACT.Identity,
                                         bias=bias_q[:, m - 1:m]).then_inc(pj_hi, 1)
                    return
                if s:
                    act.wait_ge(vt_ready, s)
                nc.scalar.activation(v_st[:, :], bank[0:HD, :], ACT.Identity, bias=bias_kv[0:HD, 0:1])
                for row in (2 * HD, 0):
                    ins = nc.scalar.activation(k_stack[row:row + HD, b, cols], bank[HD:2 * HD, :], ACT.Identity,
                                               bias=bias_kv[HD:2 * HD, 0:1])
                ins.then_inc(pj_hi, 1)

            def values(s):
                act.wait_ge(vt_ready, s + 1)
                b, c = divmod(s, NCH)
                copy(v_nat[:, b, CT * c:CT * (c + 1), :],
                     ps[:, VT, 0:CT * HD].rearrange("p (t d) -> p t d", t=CT)).then_inc(vt_done, 1)

            def piece(i):
                act.wait_ge(tern_t, i + 1)
                copy(w_T[:, i // KF, i % KF, :], ps[:, WT[i % 2], :].bitcast(f16)[:, 0:D]).then_inc(tern_done, 1)

            def total(b):
                act.wait_ge(w_in[b], 16 if b == 0 else 16 * KD)
                nc.scalar.activation(w_T[:, b, :, :], w_nat[:, b, :, :], ACT.Abs,
                                     accum_out=w_sum[:, b:b + 1]).then_inc(tern_sum, 1)

            for n in range(KD + 1):
                weight(n)
            for t in range(CT):
                token_tile(0, t)
            for n in range(KD + 1, 2 * KD + 1):
                weight(n)
            act.wait_ge(bias_in, 48)
            for what, s, a in projection_order():
                if what == "project":
                    project(s, a)
                    if s == 0 and a in (0, NM - 1):
                        total(a // (NM - 1))
                elif what == "values":
                    values(s)
                elif what == "tokens":
                    token_tile(s, a)
                elif what == "place":
                    piece(s)

            def unit(g, b, **ends):
                n = 2 * g + b
                for ev in unit_order(**ends):
                    if ev[0] == "score":
                        w = STEPS[ev[1]][3]
                        if ev[2] == 0:
                            act.wait_ge(value_done, NS * n + ev[1] + 1)
                        for h in range(2 * ev[2], 2 * ev[2] + 2):
                            at = HG * ev[1] + h
                            act.wait_ge(score_ready, ONE + NH * n + at + 1)
                            nc.scalar.activation(prob[:, ev[1] % 3, h, 0:w], ps[:, SC[at % 3], 0:w], ACT.Exp,
                                                 scale=SCALE).then_inc(exp_done, 1)
                    elif ev[0] == "sums":
                        _, c, back = ev
                        u = NCH * (n - back) + c
                        act.wait_ge(output_step, OCRED + NOUT * (u - 1))
                        act.wait_ge(value_done, PCRED + NS * (n - back) + (CT if c == 0 else NS))
                        copy(raw[:, c, :], ps[:, AC, :]).then_inc(acc_free, 1)
                        nc.scalar.activation(den[:, c, :], ps[:, DN, :], ACT.Copy, bias=1e-18).then_inc(den_free, 1)

            unit(0, 0, first=True)
            with act.Fori(0, G - 1) as g:
                unit(g, 1)
                unit(g + 1, 0)
            unit(G - 1, 1, last=True)

            def tokens2(ch):
                for t in range(CT):
                    act.wait_ge(t2_ready, ONE + CT * ch + t + 1)
                    copy(z2T_hi[:, :, t * P:(t + 1) * P],
                         ps[:, T2[t % 2], :].rearrange("p (k t) -> p k t", k=KD)).then_inc(t2_hi, 1)

            def fc(ch):
                def hi(f):
                    act.wait_ge(sq_ok, FB + KF * ch + f + 1)
                    copy(act_hi[:, f, :], sq_s[:, f % FB, :]).then_inc(act_hi_ok, 1)

                for f in range(KF):
                    act.wait_ge(fc_ready, KF * ch + f + 1)
                    act.wait_ge(sq_ok, KF * ch + f + 1)
                    nc.scalar.activation(relu_s[:, f % FB, :], ps[:, 2 + f % FB, :], ACT.Relu, scale=0.25).then_inc(relu_ok, 1)
                    if f:
                        hi(f - 1)
                hi(KF - 1)

            tokens2(0)
            with act.Fori(0, B * NCH - 1) as ch:
                fc(ch)
                tokens2(ch + 1)
            fc(B * NCH - 1)

        @block.vector
        def _(dve):
            for m in (xt_free, pj_free, t2_free, out_ok):
                dve.sem_inc(m, CRED)
            dve.sem_inc(peak_free, BCRED)
            dve.sem_inc(sq_ok, FB)
            dve.sem_inc(act_ok, ONE)

            def minus(out_ap, in_ap, hi_ap):
                return nc.vector.tensor_tensor(out_ap, in_ap, hi_ap, ALU.subtract)

            def norm_stats(src, base):
                for t in range(CT):
                    ins = nc.vector.bn_stats(stats[:, t, :], src(t))
                ins.then_inc(ln_seq, 1)
                dve.wait_ge(ln_seq, base + 1)
                dve.sem_inc(passed, 1)
                for t in range(CT):
                    ins = nc.vector.bn_aggr(moments[:, t, :], stats[:, t, :])
                ins.then_inc(ln_seq, 1)

            def norm_rstd(base):
                dve.wait_ge(ln_seq, base + 2)
                at = [base + 2]

                def step(ins):
                    at[0] += 1
                    ins.then_inc(ln_seq, 1)
                    dve.wait_ge(ln_seq, at[0])

                step(nc.vector.tensor_scalar(var[:, :], moments[:, :, 1], EPS, None, ALU.add))
                step(nc.vector.tensor_scalar(guess[:, :], var[:, :].bitcast(i32), 1, None, ALU.logical_shift_right))
                step(nc.vector.tensor_scalar(rstd[:, :].bitcast(i32), guess[:, :], -1.0, float(0x5F3759DF),
                                             ALU.mult, ALU.add))
                for _ in range(NEWTON):
                    step(nc.vector.tensor_tensor(newton[:, :], rstd[:, :], rstd[:, :], ALU.mult))
                    step(nc.vector.scalar_tensor_tensor(newton[:, :], newton[:, :], -0.5, var[:, :], ALU.mult, ALU.mult))
                    step(nc.vector.scalar_tensor_tensor(rstd[:, :], newton[:, :], 1.5, rstd[:, :], ALU.add, ALU.mult))

            def norm_apply(src, dst):
                for t in range(CT):
                    ins = nc.vector.tensor_scalar(dst(t), src(t), moments[:, t, 0:1], rstd[:, t:t + 1],
                                                  ALU.subtract, ALU.mult)
                return ins

            def norm1(s, part):
                x_of = lambda t: x_in[:, s % NCH, t, :]
                if part == 0:
                    dve.wait_ge(x_in_s[s % NCH], 16 * (s // NCH + 1))
                    norm_stats(x_of, LN * s)
                elif part == 1:
                    norm_rstd(LN * s)
                else:
                    norm_apply(x_of, x_of).then_inc(z_ready, 1)

            def weight(n):
                dve.wait_ge(wt_hi, n + 1)
                if n == KD:
                    minus(wkv_lo[:, :, :].rearrange("p k m -> p (k m)"), ps[:, WBANK[n], 0:KD * 2 * HD],
                          wkv_hi[:, :, :].rearrange("p k m -> p (k m)").bitcast(f32)).then_inc(wt_free, 1)
                else:
                    hi, lo, k = (wq_hi, wq_lo, n) if n < KD else (wo_hi, wo_lo, n - KD - 1)
                    minus(lo[:, k, :], ps[:, WBANK[n], :], hi[:, k, :].bitcast(f32)).then_inc(wt_free, 1)

            def token_tile(s, t):
                dve.wait_ge(xt_hi, CT * s + t + 1)
                cols = slice(t * P, (t + 1) * P)
                minus(zT_lo[:, s % NCH, :, cols], ps[:, TP[t % 2], :].rearrange("p (k t) -> p k t", k=KD),
                      zT_hi[:, s % NCH, :, cols].bitcast(f32)).then_inc(xt_free, 1)

            def project(s, m):
                n = NM * s + m
                b, cols, bank = s // NCH, slice(s % NCH * CW, (s % NCH + 1) * CW), ps[:, PJ[n % 2], :]
                dve.wait_ge(pj_hi, n + 1)
                if m:
                    nc.vector.scalar_tensor_tensor(q_all[:, b, 1, m - 1, cols], bank, bias_q[:, m - 1:m],
                                                   q_all[:, b, 0, m - 1, cols].bitcast(f32), ALU.add,
                                                   ALU.subtract).then_inc(pj_free, 1)
                else:
                    nc.vector.scalar_tensor_tensor(k_stack[HD:2 * HD, b, cols], bank[HD:2 * HD, :],
                                                   bias_kv[HD:2 * HD, 0:1], k_stack[0:HD, b, cols].bitcast(f32),
                                                   ALU.add, ALU.subtract).then_inc(pj_free, 1)

            def threshold(b):
                dve.wait_ge(tern_tot, b + 1)
                nc.vector.tensor_scalar(w_mean[:, b, :], ps[:, 7, b:b + 1], 1.0 / (D * F), 1e-5,
                                        ALU.mult, ALU.max).then_inc(mean_ok, 1)
                dve.wait_ge(mean_ok, b + 1)
                nc.vector.tensor_scalar(w_thr[:, b, 0:1], w_mean[:, b, :], 0.7, None, ALU.mult)
                nc.vector.tensor_scalar(w_thr[:, b, 1:2], w_mean[:, b, :], -0.7, None, ALU.mult).then_inc(tern_thr, 1)

            def piece(i):
                b = i // KF
                if i % KF == 0:
                    dve.wait_ge(tern_thr, b + 1)
                dve.wait_ge(tern_neg, i + 1)
                if i >= 2:
                    dve.wait_ge(tern_t, i - 1)
                nc.vector.scalar_tensor_tensor(w_q16[:, i % 2, :], w_nat[:, b, i % KF, :], w_thr[:, b, 0:1],
                                               w_neg[:, i % 2, :], ALU.is_gt, ALU.subtract).then_inc(tern_q, 1)

            def peak(n, k, at):
                h0, nh, i, s0, w, _ = PEAKS[k]
                c, r = divmod(i, CT)
                dve.wait_ge(peak_ready, NP * n + at + 1)
                dst = peak_b[:, h0:h0 + nh, r:r + 1] if s0 else peak_a[:, c, h0:h0 + nh, r:r + 1]
                src = ps[:, PK[at % NPK], 0:nh * w].rearrange("p (h w) -> p h w", h=nh)
                nc.vector.tensor_reduce(dst, src, AXX, ALU.max).then_inc(peak_free, 1)

            def turn(n, c, at):
                if c == 1:
                    dve.wait_ge(peak_free, BCRED + NP * n + at)
                    nc.vector.tensor_tensor(peak_a[:, 1, :, :], peak_a[:, 1, :, :], peak_b[:, :, :],
                                            ALU.max).then_inc(peaks_all, 1)
                dve.wait_ge(peak_ready, NP * n + at + 1)
                src = ps[0:HG * CT, PK[at % NPK], 0:P]
                nc.vector.tensor_scalar(peak_t[:, c, 0, :], src, -1.0, None, ALU.mult).then_inc(turned, 1)
                dve.wait_ge(turned, 2 * n + c + 1)
                nc.vector.scalar_tensor_tensor(peak_t[:, c, 1, :], src, -1.0, peak_t[:, c, 0, :].bitcast(f32), ALU.mult,
                                               ALU.subtract).then_inc(peak_free, LAST if c == NCH - 1 else 1)

            def first_peaks(kind, a, at):
                if kind == "peak":
                    peak(0, a, at)
                else:
                    turn(0, a, at)

            for part in range(3):
                norm1(0, part)
            for step, a in ((weight, 0), (weight, 1), (token_tile, 0), (token_tile, 1), (weight, 2), (token_tile, 2),
                            (token_tile, 3), (weight, 3), (weight, 4)):
                step(*((0, a) if step is token_tile else (a,)))
            for n in range(KD + 1, 2 * KD + 1):
                weight(n)
            norm1(1, 0)
            dve.wait_ge(bias_in, 48)
            for what, s, a in projection_order():
                if what == "project":
                    project(s, a)
                    if (s, a) == (0, 0):
                        norm1(1, 1)
                        norm1(1, 2)
                elif what == "sum":
                    threshold(s)
                elif what == "norm":
                    norm1(s, a)
                elif what == "tokens":
                    token_tile(s, a)
                elif what == "piece":
                    piece(s)
                elif what in ("peak", "turn"):
                    first_peaks(what, s, a)
            nc.vector.tensor_scalar(out_scale[:, 1:2], w_mean[:, 0, :], w_mean[:, 0, :], 16.0, ALU.mult,
                                    ALU.mult).then_inc(mean_ok, 1)
            dve.wait_ge(mean_ok, B + 1)
            nc.vector.tensor_tensor(out_scale[:, 0:1], out_scale[:, 1:2], w_mean[:, 1, :], ALU.mult).then_inc(mean_ok, 1)

            def attention_out(tl):
                if tl == 0:
                    dve.wait_ge(bo_in, 16)
                if tl % CT == 0:
                    dve.wait_ge(x2_in[tl // CT], 16)
                nc.vector.tensor_tensor(x2[:, tl, :], x2[:, tl, :], bo_all[:, :], ALU.add).then_inc(x2_bias, 1)
                dve.wait_ge(wo_ready, tl + 1)
                dve.wait_ge(x2_bias, tl + 1)
                nc.vector.tensor_tensor(x2[:, tl, :], ps[:, PK[tl % 2], :], x2[:, tl, :], ALU.add).then_inc(x2_ready, 1)

            def unit(g, b, **ends):
                n = 2 * g + b
                for ev in unit_order(**ends):
                    if ev[0] == "peak":
                        peak(n + 1, ev[1], ev[2])
                    elif ev[0] == "turn":
                        dve.wait_ge(peak_in[ev[1]], 32 * (n + 1))
                        turn(n + 1, ev[1], ev[2])
                    elif ev[0] == "project_out" and ev[1] % WO_TERMS == WO_TERMS - 1:
                        attention_out(ev[1] // WO_TERMS)
                    elif ev[0] == "invert":
                        invert(n, *ev[1:])

            def invert(n, part, c, back):
                cols = slice(part * CW // NINV, (part + 1) * CW // NINV)
                if part == 0:
                    dve.wait_ge(den_free, ONE + NCH * (n - back) + c + 1)
                nc.vector.reciprocal(den[:, c, cols], den[:, c, cols]).then_inc(inverted, 1)

            for at in range(EARLY_PEAKS, len(TURNS)):
                first_peaks(*TURNS[at], at)
            unit(0, 0, first=True)
            with dve.Fori(0, G - 1) as g:
                unit(g, 1)
                unit(g + 1, 0)
            unit(G - 1, 1, last=True)

            def norm2(ch, part):
                x_of = lambda t: x2[:, CT * ch + t, :]
                base = LN * B * NCH + LN * ch
                if part == 0:
                    dve.wait_ge(x2_ready, CT * (ch + 1))
                    norm_stats(x_of, base)
                elif part == 1:
                    norm_rstd(base)
                else:
                    dve.wait_ge(t2_ready, ONE + CT * ch)
                    norm_apply(x_of, lambda t: z2[:, t, :]).then_inc(z2_ready, 1)

            def token_tile2(ch, t):
                dve.wait_ge(t2_hi, CT * ch + t + 1)
                cols = slice(t * P, (t + 1) * P)
                minus(z2T_lo[:, :, cols], ps[:, T2[t % 2], :].rearrange("p (k t) -> p k t", k=KD),
                      z2T_hi[:, :, cols]).then_inc(t2_free, 1)

            def fc(ch, following):
                def lo(f):
                    dve.wait_ge(act_hi_ok, KF * ch + f + 1)
                    minus(act_lo[:, f, :], sq_s[:, f % FB, :], act_hi[:, f, :]).then_inc(act_ok, 1)

                for f in range(KF):
                    dve.wait_ge(act_ok, ONE + KF * ch + max(f - FB + 1, 0))
                    dve.wait_ge(relu_ok, KF * ch + f + 1)
                    nc.vector.scalar_tensor_tensor(sq_s[:, f % FB, :], ps[:, 2 + f % FB, :], 0.25, relu_s[:, f % FB, :],
                                                   ALU.mult, ALU.mult).then_inc(sq_ok, 1)
                    if f:
                        lo(f - 1)
                    if f == CT and following:
                        norm2(ch + 1, 0)
                lo(KF - 1)

            def output(ch, t):
                dve.wait_ge(pr_ready, CT * ch + t + 1)
                dve.wait_ge(out_in[t % 2], ONE + 16 * ((CT // 2) * ch + t // 2))
                nc.vector.scalar_tensor_tensor(out_s[:, t % 2, :], ps[:, OT[t % 2], :], out_scale[:, 0:1],
                                               x2[:, CT * ch + t, :], ALU.mult, ALU.add).then_inc(out_ok, 1)

            def outputs(ch, following):
                if following:
                    for part in (1, 2):
                        norm2(ch + 1, part)
                for what, t in FFN_OUT:
                    if what == "out":
                        output(ch, t)
                    elif following:
                        token_tile2(ch + 1, t)

            for tl in range(WO_EARLY, NT):
                attention_out(tl)
                if NORM_AT <= tl < NORM_AT + 3:
                    norm2(0, tl - NORM_AT)
                if tl > TOKENS_AT:
                    token_tile2(0, tl - TOKENS_AT - 1)
            token_tile2(0, CT - 1)
            with dve.Fori(0, B * NCH - 1) as ch:
                fc(ch, True)
                outputs(ch, True)
            fc(B * NCH - 1, False)
            outputs(B * NCH - 1, False)


_INS = ["L0_attn_q_input", "L0_attn_Wq", "L0_attn_bq", "L0_attn_Wk", "L0_attn_bk", "L0_attn_Wv", "L0_attn_bv",
        "L0_attn_Wo", "L0_attn_bo", "L0_ffn_w_fc", "L0_ffn_w_proj"]


def kernel(**inputs):
    import numpy as _np
    import concourse.bacc as _bacc
    from concourse import mybir as _mybir
    from concourse.bass_utils import run_bass_kernel_spmd as _run

    nc = _bacc.Bacc("TRN2", target_bir_lowering=False, num_devices=1)
    arrays, args = {}, []
    for name in _INS:
        a = _np.ascontiguousarray(inputs[name])
        arrays[name + "_dram"] = a
        args.append(nc.dram_tensor(name + "_dram", a.shape, _mybir.dt.from_np(a.dtype), kind="ExternalInput").ap())
    x = arrays["L0_attn_q_input_dram"]
    args.append(nc.dram_tensor("out_dram", x.shape, _mybir.dt.from_np(x.dtype), kind="ExternalOutput").ap())
    preln_layer(nc, *args)
    r = _run(nc, [arrays], core_ids=[0])
    return r.results[0]["out_dram"]
```
